# Optimizing a Trainium2 kernel written in Bass

```python
import numpy as np
import jax
import jax.numpy as jnp

def _softmax(x, axis=-1):
    return jax.nn.softmax(x, axis=axis)

def _gelu(x):
    return jax.nn.gelu(x, approximate=True)

def _silu(x):
    return jax.nn.silu(x)

def _sigmoid(x):
    return jax.nn.sigmoid(x)

def _layernorm(x, axis=-1, eps=1e-05):
    m = jnp.mean(x, axis=axis, keepdims=True)
    v = jnp.var(x, axis=axis, keepdims=True)
    return (x - m) / jnp.sqrt(v + eps)

def _scatter_add(tgt, idx, src, axis=0):
    return tgt.at[idx].add(src)

def _segment_sum(src, seg, n):
    return jax.ops.segment_sum(src, seg, n)
kernel_name = 'mk_prb_d1_jaxref_r4_1e84d6'

def setup_inputs(seed: int=0):
    np.random.seed(seed)
    _w = jnp.asarray

    def _L0_attn_setup():
        import jax, jax.numpy as jnp
        import numpy as np
        N_HEADS = 16
        HEAD_DIM = 64
        ROPE_THETA = 10000.0
        EPS = 1e-06

        def _rmsnorm(x, w):
            rms = jnp.sqrt(jnp.mean(jnp.square(x), axis=-1, keepdims=True) + EPS)
            return x / rms * w

        def _rope(x, cos, sin):
            x1, x2 = jnp.split(x, 2, axis=-1)
            return jnp.concatenate([x1 * cos - x2 * sin, x1 * sin + x2 * cos], axis=-1)
        key = jax.random.key(seed)
        ks = jax.random.split(key, 3)
        B, T, C = (2, 512, 256)
        x = jax.random.normal(ks[0], (B, T, C), dtype=jnp.float32)
        wqkv = jax.random.normal(ks[1], (3 * N_HEADS * HEAD_DIM, C), dtype=jnp.float32) * C ** (-0.5)
        wo = jax.random.normal(ks[2], (C, N_HEADS * HEAD_DIM), dtype=jnp.float32) * (N_HEADS * HEAD_DIM) ** (-0.5)
        q_norm_w = jnp.ones((HEAD_DIM,), dtype=jnp.float32)
        k_norm_w = jnp.ones((HEAD_DIM,), dtype=jnp.float32)
        return {'x': x, 'wqkv': wqkv, 'wo': wo, 'q_norm_w': q_norm_w, 'k_norm_w': k_norm_w}
    _L0_attn_in = _L0_attn_setup()

    def _L0_ffn_setup():
        import jax, jax.numpy as jnp
        import numpy as np
        B, S, H, E = (2, 2048, 256, 8)
        SCALE = 0.5
        key = jax.random.key(seed)
        k1, k2 = jax.random.split(key)
        x = jax.random.normal(k1, (B, S, H), dtype=jnp.float32)
        gate_w = jax.random.normal(k2, (E, H), dtype=jnp.float32) * 0.02
        coeff = SCALE * (1.0 + 0.05 * jnp.arange(E, dtype=jnp.float32))
        expert_w = coeff[:, None, None] * jnp.eye(H, dtype=jnp.float32)
        return {'x': x, 'gate_w': gate_w, 'expert_w': expert_w}
    _L0_ffn_in = _L0_ffn_setup()
    _d = {'L0_attn_x': _L0_attn_in['x'], 'L0_attn_wqkv': _L0_attn_in['wqkv'], 'L0_attn_wo': _L0_attn_in['wo'], 'L0_attn_q_norm_w': _L0_attn_in['q_norm_w'], 'L0_attn_k_norm_w': _L0_attn_in['k_norm_w'], 'L0_ffn_gate_w': _L0_ffn_in['gate_w'], 'L0_ffn_expert_w': _L0_ffn_in['expert_w']}
    _x0 = _d['L0_attn_x']
    _d['L0_attn_x'] = jax.random.normal(jax.random.fold_in(jax.random.key(seed), 1), (16, 512, 256), dtype=_x0.dtype)
    del _x0
    return _d

def reference(L0_attn_x, L0_attn_wqkv, L0_attn_wo, L0_attn_q_norm_w, L0_attn_k_norm_w, L0_ffn_gate_w, L0_ffn_expert_w):

    def _L0_attn_ref(x, wqkv, wo, q_norm_w, k_norm_w):
        import jax, jax.numpy as jnp
        import numpy as np
        N_HEADS = 16
        HEAD_DIM = 64
        ROPE_THETA = 10000.0
        EPS = 1e-06

        def _rmsnorm(x, w):
            rms = jnp.sqrt(jnp.mean(jnp.square(x), axis=-1, keepdims=True) + EPS)
            return x / rms * w

        def _rope(x, cos, sin):
            x1, x2 = jnp.split(x, 2, axis=-1)
            return jnp.concatenate([x1 * cos - x2 * sin, x1 * sin + x2 * cos], axis=-1)
        B, T, C = x.shape
        H, D = (N_HEADS, HEAD_DIM)
        qkv = jnp.einsum('btc,oc->bto', x, wqkv)
        q, k, v = jnp.split(qkv, 3, axis=-1)

        def to_heads(t):
            return t.reshape(B, T, H, D).transpose(0, 2, 1, 3)
        q, k, v = (to_heads(q), to_heads(k), to_heads(v))
        q = _rmsnorm(q, q_norm_w)
        k = _rmsnorm(k, k_norm_w)
        inv_freq = 1.0 / ROPE_THETA ** (jnp.arange(0, D, 2, dtype=jnp.float32) / D)
        freqs = jnp.arange(T, dtype=jnp.float32)[:, None] * inv_freq
        cos, sin = (jnp.cos(freqs), jnp.sin(freqs))
        q = _rope(q, cos, sin)
        k = _rope(k, cos, sin)
        scale = D ** (-0.5)
        attn = jnp.einsum('bhtd,bhsd->bhts', q, k) * scale
        causal = jnp.tril(jnp.ones((T, T), dtype=bool))
        attn = jnp.where(causal, attn, -jnp.inf)
        attn = jax.nn.softmax(attn.astype(jnp.float32), axis=-1).astype(q.dtype)
        out = jnp.einsum('bhts,bhsd->bhtd', attn, v)
        out = out.transpose(0, 2, 1, 3).reshape(B, T, H * D)
        return jnp.einsum('bte,ce->btc', out, wo)

    def _L0_ffn_ref(x, gate_w, expert_w):
        import jax, jax.numpy as jnp
        import numpy as np
        B, S, H, E = (2, 2048, 256, 8)
        SCALE = 0.5
        scores = jnp.einsum('bsh,eh->bse', x, gate_w)
        chosen = jnp.argmax(scores, axis=-1)
        onehot = jax.nn.one_hot(chosen, gate_w.shape[0], dtype=x.dtype)
        expert_out = jnp.einsum('bsh,efh->bsef', x, expert_w)
        return x + jnp.einsum('bsef,bse->bsf', expert_out, onehot)
    x = L0_attn_x
    xn = _layernorm(x, axis=-1)
    x = x + _L0_attn_ref(xn, L0_attn_wqkv, L0_attn_wo, L0_attn_q_norm_w, L0_attn_k_norm_w) + _L0_ffn_ref(xn, L0_ffn_gate_w, L0_ffn_expert_w)
    return x

_drawn_inputs = setup_inputs


def setup_inputs(seed=0):
    import zlib

    import numpy as np

    out = dict(_drawn_inputs(seed))
    spreads = {'L0_attn_q_norm_w': (1.0, 0.6), 'L0_attn_k_norm_w': (1.0, 0.6)}
    factors = {}
    for name, (base, spread) in spreads.items():
        noise = np.random.default_rng([zlib.crc32(name.encode()), seed]).standard_normal(out[name].shape)
        drawn = base * np.exp(spread * noise) if base else spread * noise
        out[name] = jnp.asarray(drawn.astype(out[name].dtype))
    for name, factor in factors.items():
        out[name] = (out[name] * factor).astype(out[name].dtype)
    return out
```

```python
from contextlib import ExitStack

import numpy as np

import concourse.bass as bass
from concourse import mybir
from concourse.alu_op_type import AluOpType as ALU

ACT = mybir.ActivationFunctionType
AX = mybir.AxisListType
F32 = mybir.dt.float32
F32R = mybir.dt.float32r
BF16 = mybir.dt.bfloat16
U32 = mybir.dt.uint32

P = 128
HEADS = 16
D = 64
PAIRS = HEADS // 2
SCALE = D ** -0.5
RMS_EPS = 1e-6
LN_EPS = 1e-5
MASKED = -1e30
TERMS = ((0, 0), (0, 1), (1, 0))


class Banks:

    def __init__(self, qkv, qt=None, kt=None, ot=None, proj=None, exp=None, xt=None, gate=None):
        self.qkv, self.qt, self.kt, self.ot = qkv, qt, kt, ot
        self.proj, self.exp, self.xt, self.gate = proj, exp, xt, gate


def banks(with_proj, at_end):
    if with_proj:
        return Banks(qt=0, kt=1, ot=2, proj=(2, 0), exp=(1, 2), qkv=(0, 1, 2, 0))
    if at_end:
        return Banks(qt=0, kt=1, ot=2, exp=(0, 1), xt=(2, 0), qkv=(0, 1, 2, 0), gate=1)
    return Banks(qt=0, kt=1, ot=2, exp=(0, 1), qkv=(2, 0, 1, 2))


FIRST_BANKS = Banks(xt=(2, 0), gate=0, qkv=(1, 2, 0, 1))


class Seen:

    def __init__(self, eng):
        self.eng, self.n = eng, {}

    def __call__(self, sem, by=1):
        self.n[sem] = self.n.get(sem, 0) + by
        return self.n[sem]

    def settle(self):
        for sem, n in self.n.items():
            self.eng.sem_inc(sem, -n)
        self.n = {}


def block_program(nc, x, wqkv_t, wo_t, norm_w, rope_cos, rope_sin, gate_t, expert_t, out):
    B, T, C = x.shape
    NT = T // P
    NC = C // P
    E = gate_t.shape[2]
    NI = 2 * NT
    PW = 2 * D
    assert PW == P and E == PAIRS and C == 2 * P and T == 512

    x_rows = x.rearrange("b (t p) c -> b p t c", p=P)
    out_rows = out.rearrange("b (t p) c -> b p t c", p=P)

    with ExitStack() as ctx:
        def sb(name, shape, dt=F32):
            return ctx.enter_context(nc.sbuf_tensor(name, shape, dt))

        def sem(name):
            return ctx.enter_context(nc.semaphore(name))

        w_qkv = sb("w_qkv", [P, 2, NC, PAIRS, 3 * PW], F32R)
        w_exp = sb("w_exp", [P, 2, NC, E, C], F32R)
        w_out = sb("w_out", [P, 2, PAIRS, C], F32R)
        w_gate = sb("w_gate", [P, 2, NC, E], F32R)
        t_cos = sb("t_cos", [P, NT, 2, D])
        t_sin = sb("t_sin", [P, NT, 2, D])
        nw = sb("nw", [P, 2, D])
        ident = sb("ident", [P, P])
        ident_b = sb("ident_b", [P, P], BF16)
        mask_b = sb("mask_b", [P, P], BF16)
        expert_no = sb("expert_no", [P, E])
        expert_no_i = sb("expert_no_i", [P, E], mybir.dt.int32)
        neg_half = sb("neg_half", [P, NI * 2])

        xin = sb("xin", [P, NT, C])
        xn = sb("xn", [P, NT, C])
        out_sb = xn
        res = sb("res", [P, NT, C])
        acc = sb("acc", [P, NT, C])
        xn_t = sb("xn_t", [P, 2, NC, T], F32R)
        o_t = sb("o_t", [P, 2, PAIRS, T], F32R)
        ln_stat = sb("ln_stat", [P, NT, 6])
        ln_mv = sb("ln_mv", [P, NT, 2])
        ln_ve = sb("ln_ve", [P, NT])
        ln_rstd = sb("ln_rstd", [P, NT])
        top = sb("top", [P, NT, 8])
        top_i = sb("top_i", [P, NT, 8], U32)
        chosen = sb("chosen", [P, NT])
        onehot = sb("onehot", [P, NT, E])
        scores_g = sb("scores_g", [P, NT, E])

        work = sb("work", [P, 5, NT * 2 * PW])
        qk = work[:, 0, :].rearrange("p (t n) -> p t n", t=NT)
        qk_cos = work[:, 1, :].rearrange("p (t n) -> p t n", t=NT)
        qk_sin = work[:, 2, :].rearrange("p (t n) -> p t n", t=NT)
        qk_sq = work[:, 3, :].rearrange("p (t n) -> p t n", t=NT)
        qk_rot = work[:, 4, :].rearrange("p (t n) -> p t n", t=NT)
        v = sb("v", [P, PAIRS, NT, PW])
        ss = sb("ss", [P, NT, 4])
        ms = sb("ms", [P, NT, 4])
        rms_inv = sb("rms_inv", [P, NT, 4])
        q_scale = sb("q_scale", [P, NT, 2])
        q_t = sb("q_t", [P, T])
        k_t = sb("k_t", [P, T])
        prob = sb("prob", [P, 2, T])
        prob_t = sb("prob_t", [P, 2, T])
        neg_max = sb("neg_max", [P, NT, 2])
        bias = sb("bias", [P, NT, 2])
        row_sum = sb("row_sum", [P, NT, 2])
        row_inv = sb("row_inv", [P, NT, 2])
        o_rows = prob[:, 0, :].rearrange("p (t n) -> p t n", t=NT)

        ps_g = [ctx.enter_context(nc.psum_tensor(f"ps_g{i}", [P, 512], F32)) for i in range(3)]
        ps_s = [ctx.enter_context(nc.psum_tensor(f"ps_s{i}", [P, 512], F32)) for i in range(2)]
        ps_p = [ctx.enter_context(nc.psum_tensor(f"ps_p{i}", [P, 512], F32)) for i in range(2)]
        ps_o = ctx.enter_context(nc.psum_tensor("ps_o", [P, 512], F32))

        s_consts_sp = sem("consts_sp")
        s_const_pool = sem("const_pool")
        s_const_self = sem("const_self")
        s_w_loaded0 = sem("w_loaded0")
        s_w_loaded1 = sem("w_loaded1")
        s_w_split_act = sem("w_split_act")
        s_w_free = sem("w_free")
        s_x_loaded = sem("x_loaded")
        s_x_free = sem("x_free")
        s_x_var = sem("x_var")
        s_x_rstd = sem("x_rstd")
        s_xn_pe = sem("xn_pe")
        s_xn_pool = sem("xn_pool")
        s_res_done = sem("res_done")
        s_xt_act = sem("xt_act")
        s_xnt_act = sem("xnt_act")
        s_gate_dve = sem("gate_dve")
        s_qkv_act = sem("qkv_act")
        s_qk_dve = sem("qk_dve")
        s_qk_cos_pool = sem("qk_cos_pool")
        s_ss_pool = sem("ss_pool")
        s_rms_self = sem("rms_self")
        s_qk_rot_self = sem("qk_rot_self")
        s_qk_rot_pe = sem("qk_rot_pe")
        s_qt_act = sem("qt_act")
        s_kt_dve = sem("kt_dve")
        s_ot_act = sem("ot_act")
        s_ot_dve = sem("ot_dve")
        s_exp_dve = sem("exp_dve")
        s_proj_dve = sem("proj_dve")
        s_out_ready = sem("out_ready")
        s_out_stored = sem("out_stored")
        s_out_last = sem("out_last")
        s_scores_dve = sem("scores_dve")
        s_bias_act = sem("bias_act")
        s_prob_pe = sem("prob_pe")
        s_pt_act = sem("pt_act")
        s_pt_dve = sem("pt_dve")
        s_prob_t_act = sem("prob_t_act")
        s_prob_t_dve = sem("prob_t_dve")
        s_o_dve = sem("o_dve")
        s_o_pe = sem("o_pe")
        s_dve_self = sem("dve_self")
        s_start_pe = sem("start_pe")
        w_loaded = (s_w_loaded0, s_w_loaded1)
        g_free = [sem(f"g_free{i}") for i in range(3)]

        block = ctx.enter_context(nc.Block())

        ITEMS = [(h, i) for i in (1, 3, 2, 0) for h in range(2)]
        BY_ACT = {m for m in range(NI) if m % 2 == 0}
        QKV_STEP = {1: 0, 2: 1, 3: 2, 4: 3}
        QKV_STEP_NEXT = {4: 0, 5: 1, 6: 2, 7: 3}
        XT_STEP, GATE_STEP = 1, 8

        def batches(eng, batch):
            batch(0, True, False)
            with eng.Fori(1, B - 1) as b:
                batch(b, False, False)
            batch(B - 1, False, True)

        def pairs(eng, pair):
            pair(0, PAIRS - 1, 1)
            with eng.Fori(1, PAIRS - 1) as hp:
                pair(hp, hp - 1, hp + 1)
            pair(PAIRS - 1, PAIRS - 2, 0)

        def is_int(hp, n):
            return isinstance(hp, int) and hp == n

        WCH = 2 * 3 * PW * 3

        def weight_chunks():
            yield w_gate[:, :, :, :].rearrange("p a c e -> p a (c e)"), gate_t.rearrange("p c e -> p (c e)")
            for c in range(NC):
                for hp in range(0, PAIRS, 4):
                    yield (w_qkv[:, :, c, hp:hp + 4, :].rearrange("p a h n -> p a (h n)"),
                           wqkv_t[:, c, hp:hp + 4, :].rearrange("p h n -> p (h n)"))
            for c in range(NC):
                yield (w_exp[:, :, c, :, :].rearrange("p a e n -> p a (e n)"),
                       expert_t[:, c, :, :].rearrange("p e n -> p (e n)"))
            yield (w_out[:, :, :, :].rearrange("p a h n -> p a (h n)"), wo_t.rearrange("p h n -> p (h n)"))

        @block.sync
        def _(sp):
            seen = Seen(sp)
            for dst, src in ((nw[:, :, :], norm_w), (xin[:, :, :], x_rows[0]), (t_cos[:, :, 0, :], rope_cos),
                             (t_sin[:, :, 0, :], rope_sin)):
                sp.dma_start(dst, src).then_inc(s_consts_sp, 16)
            flat = work[:, :, :].rearrange("p a n -> p (a n)")
            for n, (dst, src) in enumerate(weight_chunks()):
                if n >= 2:
                    sp.wait_ge(s_w_free, seen(s_w_free))
                size = src.free_size()
                sp.dma_start(flat[:, (n % 2) * WCH:(n % 2) * WCH + size], src)\
                    .then_inc(w_loaded[n % 2], 16)
            seen.settle()

            def batch(b, first, last):
                if not last:
                    sp.wait_ge(s_x_free, seen(s_x_free))
                    sp.dma_start(xin[:, :, :], x_rows[b + 1]).then_inc(s_x_loaded, 16)
                if not first:
                    sp.wait_ge(s_out_ready, seen(s_out_ready))
                    sp.dma_start(out_rows[b - 1], out_sb[:, :, :]).then_inc(s_out_stored, 16)
                seen.settle()

            batches(sp, batch)
            sp.wait_ge(s_out_ready, 1)
            sp.dma_start(out_rows[B - 1], out_sb[:, :, :]).then_inc(s_out_last, 16)
            sp.wait_ge(s_out_last, 16)

        @block.gpsimd
        def _(pool):
            seen = Seen(pool)
            pool.memset(ident[:, :], 0.0).then_inc(s_const_self, 1)
            pool.memset(ident_b[:, :], 0.0).then_inc(s_const_self, 1)
            pool.memset(mask_b[:, :], 0.0).then_inc(s_const_self, 1)
            pool.memset(neg_half[:, :], -0.5).then_inc(s_const_self, 1)
            pool.iota(expert_no_i[:, :], [[1, E]], base=0, channel_multiplier=0).then_inc(s_const_self, 1)
            pool.wait_ge(s_const_self, 5)
            for m in (ident, ident_b):
                pool.affine_select(out=m[:, :], in_=m[:, :], compare_op=ALU.not_equal, fill=1.0,
                                   base=0, pattern=[[-1, P]], channel_multiplier=1)
            pool.affine_select(out=mask_b[:, :], in_=mask_b[:, :], compare_op=ALU.is_ge, fill=MASKED,
                               base=0, pattern=[[-1, P]], channel_multiplier=1).then_inc(s_start_pe, 1)
            pool.tensor_copy(expert_no[:, :], expert_no_i[:, :]).then_inc(s_const_pool, 1)

            def layernorm():
                pool.wait_ge(s_x_var, seen(s_x_var))
                pool.tensor_tensor(ln_rstd[:, :], ln_ve[:, :], neg_half[:, 0:NT], ALU.pow).then_inc(s_x_rstd, 1)
                pool.wait_ge(s_xn_pool, seen(s_xn_pool))
                pool.tensor_tensor(res[:, :, :], xin[:, :, :], xn[:, :, :], ALU.add).then_inc(s_res_done, 1)

            def rotate(t):
                pool.wait_ge(s_qk_cos_pool, seen(s_qk_cos_pool))
                half = [y[:, t, :].rearrange("p (h two d) -> p h two d", two=2, d=D // 2)
                        for y in (qk_cos, qk_sin, qk_rot)]
                for a in range(2):
                    r = pool.tensor_tensor(half[2][:, :, a, :], half[0][:, :, a, :], half[1][:, :, 1 - a, :], ALU.add)
                return r

            def finish_qk(last_rot):
                last_rot.then_inc(s_qk_rot_self, 1)
                pool.wait_ge(s_ss_pool, seen(s_ss_pool))
                pool.tensor_tensor(rms_inv[:, :, :], ms[:, :, :],
                                   neg_half[:, :].rearrange("p (t n) -> p t n", t=NT), ALU.pow).then_inc(s_rms_self, 1)
                pool.wait_ge(s_rms_self, seen(s_rms_self))
                pool.wait_ge(s_qk_rot_self, seen(s_qk_rot_self))
                k_rot = qk_rot[:, :, PW:].rearrange("p t (h d) -> p t h d", d=D)
                pool.tensor_tensor(k_rot, k_rot, rms_inv[:, :, 2:4].unsqueeze(3).to_broadcast([P, NT, 2, D]), ALU.mult)\
                    .then_inc(s_qk_rot_pe, 1)

            def qkv_next():
                for t in range(NT):
                    r = rotate(t)
                finish_qk(r)

            layernorm()
            qkv_next()
            seen.settle()

            def batch(b, first, last):
                def pair(hp, hp_prev, hp_next):
                    at_end = is_int(hp, PAIRS - 1)
                    if at_end and not last:
                        layernorm()
                    if not (at_end and last):
                        qkv_next()
                    seen.settle()
                pairs(pool, pair)
            batches(pool, batch)

        @block.scalar
        def _(act):
            seen = Seen(act)

            def xt_hi(g):
                for c in range(NC):
                    act.wait_ge(s_xt_act, seen(s_xt_act))
                    act.activation(xn_t[:, 0, c, :], ps_g[g.xt[c]][:, :], ACT.Copy).then_inc(s_xnt_act, 1)

            def take_qkv(t, hp, g):
                ps = ps_g[g.qkv[t]]
                act.wait_ge(s_qkv_act, seen(s_qkv_act))
                act.activation(qk[:, t, :], ps[:, 0:2 * PW], ACT.Copy).then_inc(s_qk_dve, 1)
                act.activation(qk_sq[:, t, :], ps[:, 0:2 * PW], ACT.Square).then_inc(s_qk_dve, 1)
                act.activation(v[:, hp, t, :], ps[:, 2 * PW:3 * PW], ACT.Copy).then_inc(g_free[g.qkv[t]], 1)

            xt_hi(FIRST_BANKS)
            for t in range(NT):
                take_qkv(t, 0, FIRST_BANKS)
            seen.settle()

            def ot_hi(hp, g):
                act.wait_ge(s_ot_act, seen(s_ot_act))
                act.activation(o_t[:, 0, hp, :], ps_g[g.ot][:, :], ACT.Copy).then_inc(s_ot_dve, 1)

            def batch(b, first, last):
                def pair(hp, hp_prev, hp_next):
                    at_start, at_end = is_int(hp, 0), is_int(hp, PAIRS - 1)
                    g = banks(at_start and not first, at_end)
                    act.wait_ge(s_qt_act, seen(s_qt_act))
                    act.activation(q_t[:, :], ps_g[g.qt][:, :], ACT.Copy).then_inc(g_free[g.qt], 1)
                    if not (at_start and first):
                        ot_hi(hp_prev, g)
                    steps = QKV_STEP_NEXT if at_end else QKV_STEP
                    for step in range(NI + 2):
                        if step < NI:
                            h, i = ITEMS[step]
                            act.wait_ge(s_bias_act, seen(s_bias_act))
                            act.activation(prob[:, step % 2, 0:(i + 1) * P], ps_s[step % 2][:, 0:(i + 1) * P], ACT.Exp,
                                           bias=bias[:, i, h:h + 1], scale=q_scale[:, i, h:h + 1],
                                           accum_out=row_sum[:, i, h:h + 1]).then_inc(s_prob_pe, 1)
                        if at_end and not last and step == XT_STEP:
                            xt_hi(g)
                        if step in steps and not (at_end and last):
                            take_qkv(steps[step], hp_next, g)
                        m = step - 1
                        if m in BY_ACT:
                            w = (ITEMS[m][1] + 1) * P
                            act.wait_ge(s_pt_act, seen(s_pt_act))
                            act.activation(prob_t[:, m % 2, 0:w], ps_p[m % 2][:, 0:w], ACT.Copy).then_inc(s_prob_t_act, 1)
                    seen.settle()
                pairs(act, pair)

            batches(act, batch)
            ot_hi(PAIRS - 1, banks(True, False))

        @block.tensor
        def _(pe):
            seen = Seen(pe)

            def product(ps, lhs, rhs, parts=NC):
                n = 0
                for c in range(parts):
                    for a, b in TERMS:
                        r = pe.matmul(ps, lhs(a, c), rhs(b, c), start=(n == 0), stop=(n == 3 * parts - 1))
                        n += 1
                return r

            def bank(i):
                pe.wait_ge(g_free[i], seen(g_free[i]))
                return ps_g[i]

            def xt(g):
                pe.wait_ge(s_xn_pe, seen(s_xn_pe))
                for c in range(NC):
                    ps = bank(g.xt[c])
                    for t in range(NT):
                        r = pe.transpose(ps[:, t * P:(t + 1) * P], xn[:, t, c * P:(c + 1) * P], ident[:, :])
                    r.then_inc(s_xt_act, 1)

            def gate(g):
                ps = bank(g.gate)
                for t in range(NT):
                    rows = slice(t * P, (t + 1) * P)
                    r = product(ps[:, t * E:(t + 1) * E], lambda a, c: xn_t[:, a, c, rows], lambda b, c: w_gate[:, b, c, :])
                r.then_inc(s_gate_dve, 1)

            def qkv(t, hp, g):
                rows = slice(t * P, (t + 1) * P)
                product(bank(g.qkv[t])[:, 0:3 * PW], lambda a, c: xn_t[:, a, c, rows], lambda b, c: w_qkv[:, b, c, hp, :])\
                    .then_inc(s_qkv_act, 1)

            def experts(hp, g):
                for half in range(2):
                    ps = bank(g.exp[half])
                    for t in (2 * half, 2 * half + 1):
                        rows = slice(t * P, (t + 1) * P)
                        r = product(ps[:, (t % 2) * C:(t % 2 + 1) * C], lambda a, c: xn_t[:, a, c, rows],
                                    lambda b, c: w_exp[:, b, c, hp, :])
                    r.then_inc(s_exp_dve, 1)

            def ot(g):
                pe.wait_ge(s_o_pe, seen(s_o_pe))
                ps = bank(g.ot)
                for t in range(NT):
                    r = pe.transpose(ps[:, t * P:(t + 1) * P], o_rows[:, t, :], ident[:, :])
                r.then_inc(s_ot_act, 1)

            def proj(g):
                for half in range(2):
                    ps = bank(g.proj[half])
                    for t in (2 * half, 2 * half + 1):
                        rows = slice(t * P, (t + 1) * P)
                        r = product(ps[:, (t % 2) * C:(t % 2 + 1) * C], lambda a, c: o_t[:, a, c, rows],
                                    lambda b, c: w_out[:, b, c, :], PAIRS)
                    r.then_inc(s_proj_dve, 1)

            for i in range(3):
                pe.sem_inc(g_free[i], 1)
            pe.wait_ge(s_start_pe, seen(s_start_pe))
            pe.wait_ge(s_w_split_act, seen(s_w_split_act))
            xt(FIRST_BANKS)
            gate(FIRST_BANKS)
            for t in range(NT):
                qkv(t, 0, FIRST_BANKS)
            seen.settle()

            def scores(m):
                h, i = ITEMS[m]
                rows, w = slice(h * D, (h + 1) * D), (i + 1) * P
                ps = ps_s[m % 2]
                pe.matmul(ps[:, 0:w], q_t[rows, i * P:w], k_t[rows, 0:w], start=True, stop=True)
                pe.matmul(ps[:, i * P:w], ident_b[:, :], mask_b[:, :], start=False, stop=True,
                          skip_group_check=True).then_inc(s_scores_dve, 1)

            def transpose_probs(m):
                h, i = ITEMS[m]
                pe.wait_ge(s_prob_pe, seen(s_prob_pe))
                for j in range(i + 1):
                    r = pe.transpose(ps_p[m % 2][:, j * P:(j + 1) * P], prob[:, m % 2, j * P:(j + 1) * P], ident[:, :])
                r.then_inc(s_pt_act if m in BY_ACT else s_pt_dve, 1)

            def values(m, hp):
                h, i = ITEMS[m]
                ready = s_prob_t_act if m in BY_ACT else s_prob_t_dve
                pe.wait_ge(ready, seen(ready))
                at = i * PW + h * D
                for j in range(i + 1):
                    r = pe.matmul(ps_o[:, at:at + D], prob_t[:, m % 2, j * P:(j + 1) * P],
                                  v[:, hp, j, h * D:(h + 1) * D], start=(j == 0), stop=(j == i))
                return r

            def batch(b, first, last):
                def pair(hp, hp_prev, hp_next):
                    at_start, at_end = is_int(hp, 0), is_int(hp, PAIRS - 1)
                    g = banks(at_start and not first, at_end)
                    pe.wait_ge(s_qk_rot_pe, seen(s_qk_rot_pe))
                    for n, (i, done) in enumerate(((g.qt, s_qt_act), (g.kt, s_kt_dve))):
                        ps = bank(i)
                        for t in range(NT):
                            r = pe.transpose(ps[:, t * P:(t + 1) * P], qk_rot[:, t, n * PW:(n + 1) * PW], ident[:, :])
                        r.then_inc(done, 1)
                    if not (at_start and first):
                        ot(g)
                    if at_start and not first:
                        proj(g)
                    experts(hp, g)
                    steps = QKV_STEP_NEXT if at_end else QKV_STEP
                    for step in range(NI + 2):
                        if step < NI:
                            scores(step)
                        if at_end and not last:
                            if step == XT_STEP:
                                xt(g)
                        if step in steps and not (at_end and last):
                            qkv(steps[step], hp_next, g)
                        if at_end and not last and step == GATE_STEP:
                            gate(g)
                        if 1 <= step <= NI:
                            transpose_probs(step - 1)
                        if step >= 2:
                            r = values(step - 2, hp)
                    r.then_inc(s_o_dve, 1)
                    seen.settle()
                pairs(pe, pair)

            batches(pe, batch)
            ot(banks(True, False))
            proj(banks(True, False))

        @block.vector
        def _(dve):
            seen = Seen(dve)

            def own(r):
                r.then_inc(s_dve_self, 1)
                dve.wait_ge(s_dve_self, seen(s_dve_self))

            def split(hi, lo, src, signal):
                own(dve.tensor_copy(hi, src))
                dve.tensor_tensor(lo, src, hi.bitcast(F32), ALU.subtract).then_inc(signal, 1)

            def layernorm():
                for t in range(NT):
                    r = dve.bn_stats(ln_stat[:, t, :], xin[:, t, :])
                own(r)
                for t in range(NT):
                    r = dve.bn_aggr(ln_mv[:, t, :], ln_stat[:, t, :])
                own(r)
                dve.tensor_scalar(ln_ve[:, :], ln_mv[:, :, 1], LN_EPS, None, ALU.add).then_inc(s_x_var, 1)
                dve.wait_ge(s_x_rstd, seen(s_x_rstd))
                for t in range(NT):
                    r = dve.tensor_scalar(xn[:, t, :], xin[:, t, :], ln_mv[:, t, 0:1], ln_rstd[:, t:t + 1],
                                          ALU.subtract, ALU.mult)
                r.then_inc(s_xn_pe, 1)
                dve.drain().then_inc(s_xn_pool, 1)

            def xt_lo(g):
                for c in range(NC):
                    dve.wait_ge(s_xnt_act, seen(s_xnt_act))
                    dve.tensor_tensor(xn_t[:, 1, c, :], ps_g[g.xt[c]][:, :], xn_t[:, 0, c, :].bitcast(F32), ALU.subtract)\
                        .then_inc(g_free[g.xt[c]], 1)

            def choose(g):
                dve.wait_ge(s_gate_dve, seen(s_gate_dve))
                own(dve.tensor_copy(scores_g[:, :, :], ps_g[g.gate][:, 0:NT * E].rearrange("p (t e) -> p t e", t=NT)))
                for t in range(NT):
                    r = dve.max(top[:, t, :], scores_g[:, t, :])
                    if t == 0:
                        r.then_inc(g_free[g.gate], 1)
                own(r)
                for t in range(NT):
                    r = dve.max_index(top_i[:, t, :], top[:, t, :], scores_g[:, t, :])
                own(r)
                own(dve.tensor_copy(chosen[:, :], top_i[:, :, 0]))
                for t in range(NT):
                    r = dve.tensor_scalar(onehot[:, t, :], expert_no[:, :], chosen[:, t:t + 1], None, ALU.is_equal)
                own(r)

            def rope_products(t):
                dve.wait_ge(s_qk_dve, seen(s_qk_dve))
                src = qk[:, t, :].rearrange("p (n h d) -> p n h d", n=2, h=2)
                for dst, table in ((qk_cos, t_cos), (qk_sin, t_sin)):
                    r = dve.tensor_tensor(dst[:, t, :].rearrange("p (n h d) -> p n h d", n=2, h=2), src,
                                          table[:, t, :, :].unsqueeze(2).to_broadcast([P, 2, 2, D]), ALU.mult)
                r.then_inc(s_qk_cos_pool, 1)
                dve.wait_ge(s_qk_dve, seen(s_qk_dve))
                return dve.tensor_reduce(ss[:, t, :], qk_sq[:, t, :].rearrange("p (n d) -> p n d", d=D), AX.X, ALU.add)

            def mean_square(r):
                own(r)
                dve.tensor_scalar(ms[:, :, :], ss[:, :, :], 1.0 / D, RMS_EPS, ALU.mult, ALU.add).then_inc(s_ss_pool, 1)

            dve.wait_ge(s_consts_sp, 64)
            layernorm()
            dve.wait_ge(s_const_pool, 1)
            own(dve.tensor_copy(t_cos[:, :, 1, :], t_cos[:, :, 0, :]))
            own(dve.tensor_copy(t_sin[:, :, 1, :], t_sin[:, :, 0, :]))
            for t in range(NT):
                for table in (t_cos, t_sin):
                    dve.tensor_tensor(table[:, t, :, :], table[:, t, :, :], nw[:, :, :], ALU.mult)
            flat = work[:, :, :].rearrange("p a n -> p (a n)")
            for n, (dst, src) in enumerate(weight_chunks()):
                size = src.free_size()
                dve.wait_ge(w_loaded[n % 2], seen(w_loaded[n % 2], 16))
                split(dst[:, 0, :], dst[:, 1, :], flat[:, (n % 2) * WCH:(n % 2) * WCH + size], s_w_free)
            own(dve.memset(bias[:, :, :], 0.0))
            dve.memset(neg_max[:, :, :], 0.0).then_inc(s_w_split_act, 1)

            xt_lo(FIRST_BANKS)
            choose(FIRST_BANKS)
            for t in range(NT):
                r = rope_products(t)
            mean_square(r)
            seen.settle()

            def ot_lo(hp, g):
                dve.wait_ge(s_ot_dve, seen(s_ot_dve))
                dve.tensor_tensor(o_t[:, 1, hp, :], ps_g[g.ot][:, :], o_t[:, 0, hp, :].bitcast(F32), ALU.subtract)\
                    .then_inc(g_free[g.ot], 1)

            def output(g):
                for half in range(2):
                    dve.wait_ge(s_proj_dve, seen(s_proj_dve))
                    rows = slice(2 * half, 2 * half + 2)
                    dve.tensor_tensor(out_sb[:, rows, :], ps_g[g.proj[half]][:, :].rearrange("p (t c) -> p t c", c=C),
                                      acc[:, rows, :], ALU.add).then_inc(g_free[g.proj[half]], 1)

            def batch(b, first, last):
                def pair(hp, hp_prev, hp_next):
                    at_start, at_end = is_int(hp, 0), is_int(hp, PAIRS - 1)
                    g = banks(at_start and not first, at_end)
                    if at_start:
                        dve.wait_ge(s_res_done, seen(s_res_done))
                    dve.wait_ge(s_kt_dve, seen(s_kt_dve))
                    r = dve.tensor_scalar(q_scale[:, :, :], rms_inv[:, :, 0:2], SCALE, None, ALU.mult)
                    if at_start and not last:
                        r.then_inc(s_x_free, 1)
                    dve.tensor_copy(k_t[:, :], ps_g[g.kt][:, :]).then_inc(g_free[g.kt], 1)
                    if not (at_start and first):
                        ot_lo(hp_prev, g)
                    if at_start and not first:
                        output(g)
                        own(dve.drain())
                    for half in range(2):
                        dve.wait_ge(s_exp_dve, seen(s_exp_dve))
                        ps = ps_g[g.exp[half]]
                        for t in (2 * half, 2 * half + 1):
                            r = dve.scalar_tensor_tensor(acc[:, t, :], ps[:, (t % 2) * C:(t % 2 + 1) * C],
                                                         onehot[:, t, bass.ds(hp, 1)],
                                                         res[:, t, :] if at_start else acc[:, t, :],
                                                         ALU.mult, ALU.add)
                            if at_start and not first and t == 0:
                                r.then_inc(s_out_ready, 1)
                        r.then_inc(g_free[g.exp[half]], 1)
                    steps = QKV_STEP_NEXT if at_end else QKV_STEP
                    if at_end and not last:
                        dve.wait_ge(s_x_loaded, seen(s_x_loaded, 16))
                        if not first:
                            dve.wait_ge(s_out_stored, seen(s_out_stored, 16))
                        layernorm()
                    for step in range(NI + 2):
                        if step < NI:
                            h, i = ITEMS[step]
                            dve.wait_ge(s_scores_dve, seen(s_scores_dve))
                            own(dve.tensor_reduce(neg_max[:, i, h:h + 1], ps_s[step % 2][:, 0:(i + 1) * P],
                                                  AX.X, ALU.max, negate=True))
                            dve.tensor_tensor(bias[:, i, h:h + 1], neg_max[:, i, h:h + 1], q_scale[:, i, h:h + 1],
                                              ALU.mult).then_inc(s_bias_act, 1)
                        if at_end and not last and step == XT_STEP:
                            xt_lo(g)
                        m = step - 1
                        if 0 <= m < NI and m not in BY_ACT:
                            w = (ITEMS[m][1] + 1) * P
                            dve.wait_ge(s_pt_dve, seen(s_pt_dve))
                            dve.tensor_copy(prob_t[:, m % 2, 0:w], ps_p[m % 2][:, 0:w]).then_inc(s_prob_t_dve, 1)
                        if step in steps and not (at_end and last):
                            r = rope_products(steps[step])
                            if steps[step] == NT - 1:
                                mean_square(r)
                        if at_end and not last and step == GATE_STEP:
                            choose(g)
                    dve.wait_ge(s_o_dve, seen(s_o_dve))
                    own(dve.reciprocal(row_inv[:, :, :], row_sum[:, :, :]))
                    dve.tensor_tensor(o_rows[:, :, :].rearrange("p t (h d) -> p (t h) d", d=D),
                                      ps_o[:, :].rearrange("p (n d) -> p n d", d=D),
                                      row_inv[:, :, :].rearrange("p t h -> p (t h)").unsqueeze(2).to_broadcast([P, NI, D]),
                                      ALU.mult).then_inc(s_o_pe, 1)
                    seen.settle()
                pairs(dve, pair)

            batches(dve, batch)
            g = banks(True, False)
            ot_lo(PAIRS - 1, g)
            dve.wait_ge(s_out_stored, seen(s_out_stored, 16))
            output(g)
            dve.drain().then_inc(s_out_ready, 1)


def rope_tables(T, half):
    f = np.float32
    expo = (np.arange(0, 2 * half, 2, dtype=f) / f(2 * half)).astype(np.float64)
    inv = (1.0 / (10000.0 ** expo).astype(f).astype(np.float64)).astype(f)
    ang = (np.arange(T, dtype=f)[:, None] * inv).astype(np.float64)
    return np.cos(ang).astype(f), np.sin(ang).astype(f)


def kernel(**inputs):
    import concourse.bacc as bacc
    from concourse.bass_utils import run_bass_kernel_spmd

    x = np.ascontiguousarray(inputs["L0_attn_x"])
    B, T, C = x.shape
    nt, ncp = T // P, C // P
    wqkv = np.asarray(inputs["L0_attn_wqkv"])
    wqkv_t = wqkv.reshape(3, PAIRS, 2 * D, ncp, P).transpose(4, 3, 1, 0, 2).reshape(P, ncp, PAIRS, 6 * D)
    wo_t = np.asarray(inputs["L0_attn_wo"]).reshape(C, PAIRS, 2 * D).transpose(2, 1, 0)
    gate_w = np.asarray(inputs["L0_ffn_gate_w"])
    gate_t = gate_w.reshape(-1, ncp, P).transpose(2, 1, 0)
    expert_t = np.asarray(inputs["L0_ffn_expert_w"]).reshape(-1, C, ncp, P).transpose(3, 2, 0, 1)
    norm_w = np.stack([np.asarray(inputs["L0_attn_q_norm_w"]), np.asarray(inputs["L0_attn_k_norm_w"])])
    norm_w = np.broadcast_to(norm_w, (P, 2, D))
    cos, sin = rope_tables(T, D // 2)
    rope_cos = np.concatenate([cos, cos], 1).reshape(nt, P, D).transpose(1, 0, 2)
    rope_sin = np.concatenate([sin, -sin], 1).reshape(nt, P, D).transpose(1, 0, 2)

    arrays = {
        "x": x, "wqkv_t": wqkv_t, "wo_t": wo_t, "norm_w": norm_w, "rope_cos": rope_cos, "rope_sin": rope_sin,
        "gate_t": gate_t, "expert_t": expert_t,
    }
    arrays = {f"in_{k}": np.ascontiguousarray(a) for k, a in arrays.items()}
    nc = bacc.Bacc("TRN2", target_bir_lowering=False, num_devices=1)
    args = [nc.dram_tensor(k, a.shape, mybir.dt.from_np(a.dtype), kind="ExternalInput").ap() for k, a in arrays.items()]
    args.append(nc.dram_tensor("out", x.shape, F32, kind="ExternalOutput").ap())
    block_program(nc, *args)
    r = run_bass_kernel_spmd(nc, [arrays], core_ids=[0])
    return r.results[0]["out"]
```

```python
from contextlib import ExitStack

import numpy as np

import concourse.bass as bass
from concourse import mybir
from concourse.alu_op_type import AluOpType as ALU

ACT = mybir.ActivationFunctionType
AX = mybir.AxisListType
F32 = mybir.dt.float32
F32R = mybir.dt.float32r
BF16 = mybir.dt.bfloat16
U32 = mybir.dt.uint32

P = 128
HEADS = 16
D = 64
HEADS_OF_PAIR = 2
PAIRS = HEADS // HEADS_OF_PAIR
SCALE = D ** -0.5
RMS_EPS = 1e-6
LN_EPS = 1e-5
MASKED = -1e30
TERMS = ((0, 0), (0, 1), (1, 0))


class Banks:

    def __init__(self, qkv, qt=None, kt=None, ot=None, proj=None, exp=None, xt=None):
        self.qkv, self.qt, self.kt, self.ot = qkv, qt, kt, ot
        self.proj, self.exp, self.xt = proj, exp, xt


PAIR_BANKS = Banks(qkv=(0, 2, 0, 2), ot=1, exp=(0, 1, 0, 1), qt=2, kt=0)
LAST_PAIR_BANKS = Banks(exp=(0, 2, 0, 2), ot=1, xt=(0, 2), qkv=(0, 2, 0, 2), proj=(0, 1), qt=2, kt=0)
QK_BANKS = (PAIR_BANKS.qt, PAIR_BANKS.kt)
OWN_OT = Banks(qkv=None, ot=2)
QKV_STEPS = {0: 0, 1: 1, 2: 2, 3: 3}
EXPERT_STEPS = {4: 0, 5: 1, 8: 2}
LAST_EXPERT_STEPS = {0: 0, 1: 1, 2: 2, 3: 3}
XT_STEP = 4
PROJECT_STEP = 5
LAST_QKV_STEPS = {5: 0, 6: 1, 7: 2, 8: 3}
STATS_STEPS = {0: (0, 1), 1: (2, 3)}
NORM_STEP = 2
OT_STEP = 2
ITEMS = [(h, i) for i in (1, 3, 2, 0) for h in range(2)]
STEPS = len(ITEMS) + 2
BY_ACT = (0, 2, 3, 4, 6)


class Seen:

    def __init__(self, eng):
        self.eng, self.n = eng, {}

    def __call__(self, sem, by=1):
        self.n[sem] = self.n.get(sem, 0) + by
        return self.n[sem]

    def settle(self):
        for sem, n in self.n.items():
            self.eng.sem_inc(sem, -n)
        self.n = {}


def block_program(nc, x, wqkv_t, wo_t, norm_w, rope_cos, rope_sin, expert_t, out):
    B, T, C = x.shape
    NT = T // P
    NC = C // P
    E = expert_t.shape[2]
    NI = HEADS_OF_PAIR * NT
    PW = 2 * D
    assert PW == P and E == PAIRS and C == 2 * P and T == 512

    x_rows = x.rearrange("b (t p) c -> b p t c", p=P)
    out_rows = out.rearrange("b (t p) c -> b p t c", p=P)

    with ExitStack() as ctx:
        def sb(name, shape, dt=F32):
            return ctx.enter_context(nc.sbuf_tensor(name, shape, dt))

        def sem(name):
            return ctx.enter_context(nc.semaphore(name))

        w_qkv = sb("w_qkv", [P, 2, NC, E + PAIRS * 3 * PW], F32R)
        w_exp = sb("w_exp", [P, 2, NC, E, C], F32R)
        w_out = sb("w_out", [P, 2, PAIRS, C], F32R)
        t_cos = sb("t_cos", [P, NT, 2, D])
        t_sin = sb("t_sin", [P, NT, 2, D])
        nw = sb("nw", [P, 2, D])
        ident = sb("ident", [P, P])
        ident_b = sb("ident_b", [P, P], BF16)
        mask_b = sb("mask_b", [P, P], BF16)
        expert_no = sb("expert_no", [P, E])
        expert_no_i = sb("expert_no_i", [P, E], mybir.dt.int32)
        neg_half = sb("neg_half", [P, NI * 2])

        xin = sb("xin", [P, NT, C])
        xn = sb("xn", [P, NT, C])
        out_sb = xn
        res = sb("res", [P, NT, C])
        acc = sb("acc", [P, NT, C])
        xn_t = sb("xn_t", [P, 2, NC, T], F32R)
        o_t = sb("o_t", [P, 2, PAIRS, T], F32R)
        ln_stat = sb("ln_stat", [P, NT, 6])
        ln_mv = sb("ln_mv", [P, NT, 2])
        ln_ve = sb("ln_ve", [P, NT])
        ln_rstd = sb("ln_rstd", [P, NT])
        top = sb("top", [P, NT, 8])
        top_i = sb("top_i", [P, NT, 8], U32)
        chosen = sb("chosen", [P, NT])
        onehot = sb("onehot", [P, NT, E])
        scores_g = sb("scores_g", [P, NT, E])

        work = sb("work", [P, 4, NT * 2 * PW])
        qk = work[:, 0, :].rearrange("p (t n) -> p t n", t=NT)
        qk_cos = work[:, 1, :].rearrange("p (t n) -> p t n", t=NT)
        qk_sin = work[:, 2, :].rearrange("p (t n) -> p t n", t=NT)
        qk_rot = work[:, 3, :].rearrange("p (t n) -> p t n", t=NT)
        qk_sq = sb("qk_sq", [P, 2, 2 * PW])
        v = sb("v", [P, PAIRS, NT, PW])
        ss = sb("ss", [P, NT, 4])
        ms = sb("ms", [P, NT, 4])
        rms_inv = sb("rms_inv", [P, NT, 4])
        q_scale = sb("q_scale", [P, NT, 2])
        q_t = sb("q_t", [P, T])
        k_t = sb("k_t", [P, T])
        prob = sb("prob", [P, 2, T])
        prob_t = sb("prob_t", [P, 2, T])
        neg_max = sb("neg_max", [P, NT, 2])
        bias = sb("bias", [P, NT, 2])
        row_sum = sb("row_sum", [P, NT, 2])
        row_inv = sb("row_inv", [P, NT, 2])
        o_rows = sb("o_rows", [P, NT, PW])

        ps_g = [ctx.enter_context(nc.psum_tensor(f"ps_g{i}", [P, 512], F32)) for i in range(3)]
        ps_s = [ctx.enter_context(nc.psum_tensor(f"ps_s{i}", [P, 512], F32)) for i in range(2)]
        ps_p = [ctx.enter_context(nc.psum_tensor(f"ps_p{i}", [P, 512], F32)) for i in range(2)]
        ps_o = ctx.enter_context(nc.psum_tensor("ps_o", [P, 512], F32))

        s_consts_dve = sem("s_consts_dve")
        s_iota_dve = sem("s_iota_dve")
        s_pool_self = sem("s_pool_self")
        s_masks_pe = sem("s_masks_pe")
        s_weights_pe = sem("s_weights_pe")
        w_loaded = [sem(f"w_loaded{i}") for i in range(2)]
        s_w_free = sem("s_w_free")
        s_x_loaded = sem("s_x_loaded")
        s_x_free = sem("s_x_free")
        s_var_pool = sem("s_var_pool")
        s_rstd_dve = sem("s_rstd_dve")
        s_xn_pe = sem("s_xn_pe")
        s_xn_pool = sem("s_xn_pool")
        s_res_dve = sem("s_res_dve")
        s_xt_act = sem("s_xt_act")
        s_xt_hi_dve = sem("s_xt_hi_dve")
        s_gate_dve = sem("s_gate_dve")
        s_qkv_act = sem("s_qkv_act")
        s_qk_dve = sem("s_qk_dve")
        s_sq_free = sem("s_sq_free")
        s_products_pool = sem("s_products_pool")
        s_ms_pool = sem("s_ms_pool")
        s_rot_pe = sem("s_rot_pe")
        s_qt_act = sem("s_qt_act")
        s_kt_dve = sem("s_kt_dve")
        s_scores_dve = sem("s_scores_dve")
        s_bias_act = sem("s_bias_act")
        s_prob_pe = sem("s_prob_pe")
        s_pt_act = sem("s_pt_act")
        s_pt_dve = sem("s_pt_dve")
        s_prob_t_act = sem("s_prob_t_act")
        s_prob_t_dve = sem("s_prob_t_dve")
        s_expert_dve = sem("s_expert_dve")
        s_o_dve = sem("s_o_dve")
        s_o_pe = sem("s_o_pe")
        s_ot_act = sem("s_ot_act")
        s_ot_hi_dve = sem("s_ot_hi_dve")
        s_proj_dve = sem("s_proj_dve")
        s_dve_self = sem("s_dve_self")
        s_out_ready = sem("s_out_ready")
        s_out_stored = sem("s_out_stored")
        s_out_last = sem("s_out_last")
        g_free = [sem(f"g_free{i}") for i in range(3)]

        block = ctx.enter_context(nc.Block())

        def batches(eng, batch):
            with eng.Fori(0, B - 1) as b:
                batch(b, False)
            batch(B - 1, True)

        def pairs(eng, pair, seen):
            pair(0, "first", PAIRS - 1, 1)
            seen.settle()
            with eng.Fori(0, PAIRS // 2 - 1) as n:
                pair(n * 2 + 1, "inner", n * 2, n * 2 + 2)
                pair(n * 2 + 2, "inner", n * 2 + 1, n * 2 + 3)
                seen.settle()
            pair(PAIRS - 1, "last", PAIRS - 2, 0)
            seen.settle()

        def gate_cols(hp):
            return E if isinstance(hp, int) and hp == 0 else 0

        def plan(kind, last):
            if kind != "last":
                return PAIR_BANKS, EXPERT_STEPS, QKV_STEPS
            return LAST_PAIR_BANKS, LAST_EXPERT_STEPS, {} if last else LAST_QKV_STEPS

        chunk = 2 * P * NT * 2
        staged = work[:, :, :].rearrange("p a n -> p (a n)")

        def weight_chunks():
            cols = PAIRS * 3 * PW // 2
            for c in range(NC):
                for at, n in ((0, E + cols), (E + cols, cols)):
                    yield w_qkv[:, :, c, at:at + n], wqkv_t[:, c, at:at + n]
            for c in range(NC):
                yield (w_exp[:, :, c, :, :].rearrange("p a e n -> p a (e n)"),
                       expert_t[:, c, :, :].rearrange("p e n -> p (e n)"))
            yield (w_out[:, :, :, :].rearrange("p a h n -> p a (h n)"), wo_t.rearrange("p h n -> p (h n)"))

        @block.sync
        def _(sp):
            seen = Seen(sp)
            for dst, src in ((xin[:, :, :], x_rows[0]), (nw[:, :, :], norm_w), (t_cos[:, :, 0, :], rope_cos),
                             (t_sin[:, :, 0, :], rope_sin)):
                sp.dma_start(dst, src).then_inc(s_consts_dve, 16)
            for n, (dst, src) in enumerate(weight_chunks()):
                if n >= 2:
                    sp.wait_ge(s_w_free, seen(s_w_free))
                at = (n % 2) * chunk
                sp.dma_start(staged[:, at:at + src.free_size()], src).then_inc(w_loaded[n % 2], 16)
            sp.sem_inc(s_out_stored, 16)
            seen.settle()

            def batch(b, last):
                if not last:
                    sp.wait_ge(s_x_free, seen(s_x_free))
                    sp.dma_start(xin[:, :, :], x_rows[b + 1]).then_inc(s_x_loaded, 16)
                sp.wait_ge(s_out_ready, seen(s_out_ready))
                sp.dma_start(out_rows[b], out_sb[:, :, :]).then_inc(s_out_last if last else s_out_stored, 16)
                seen.settle()

            batches(sp, batch)
            sp.wait_ge(s_out_last, 16)

        @block.gpsimd
        def _(pool):
            seen = Seen(pool)
            pool.memset(ident[:, :], 0.0)
            pool.memset(ident_b[:, :], 0.0)
            pool.memset(mask_b[:, :], 0.0)
            pool.memset(neg_half[:, :], -0.5)
            pool.iota(expert_no_i[:, :], [[1, E]], base=0, channel_multiplier=0).then_inc(s_pool_self, 1)
            pool.wait_ge(s_pool_self, seen(s_pool_self))
            for m in (ident, ident_b):
                pool.affine_select(out=m[:, :], in_=m[:, :], compare_op=ALU.not_equal, fill=1.0,
                                   base=0, pattern=[[-1, P]], channel_multiplier=1)
            pool.affine_select(out=mask_b[:, :], in_=mask_b[:, :], compare_op=ALU.is_ge, fill=MASKED,
                               base=0, pattern=[[-1, P]], channel_multiplier=1).then_inc(s_masks_pe, 1)
            pool.tensor_copy(expert_no[:, :], expert_no_i[:, :]).then_inc(s_iota_dve, 1)

            def layernorm():
                pool.wait_ge(s_var_pool, seen(s_var_pool))
                pool.tensor_tensor(ln_rstd[:, :], ln_ve[:, :], neg_half[:, 0:NT], ALU.pow).then_inc(s_rstd_dve, 1)
                pool.wait_ge(s_xn_pool, seen(s_xn_pool))
                pool.tensor_tensor(res[:, :, :], xin[:, :, :], xn[:, :, :], ALU.add).then_inc(s_res_dve, 1)

            def rotate_next():
                for t in range(NT):
                    cos, sin, rot = [y[:, t, :].rearrange("p (h two d) -> p h two d", two=2, d=D // 2)
                                     for y in (qk_cos, qk_sin, qk_rot)]
                    pool.wait_ge(s_products_pool, seen(s_products_pool))
                    for a in range(2):
                        r = pool.tensor_tensor(rot[:, :, a, :], cos[:, :, a, :], sin[:, :, 1 - a, :], ALU.add)
                pool.wait_ge(s_ms_pool, seen(s_ms_pool))
                pool.tensor_tensor(rms_inv[:, :, :], ms[:, :, :], neg_half[:, :].rearrange("p (t n) -> p t n", t=NT),
                                   ALU.pow).then_inc(s_pool_self, 1)
                pool.wait_ge(s_pool_self, seen(s_pool_self))
                k_rot = qk_rot[:, :, PW:].rearrange("p t (h d) -> p t h d", d=D)
                pool.tensor_tensor(k_rot, k_rot, rms_inv[:, :, 2:4].unsqueeze(3).to_broadcast([P, NT, 2, D]), ALU.mult)\
                    .then_inc(s_rot_pe, 1)

            layernorm()
            rotate_next()
            seen.settle()

            def batch(b, last):
                def pair(hp, kind, hp_prev, hp_next):
                    if kind == "last" and last:
                        return
                    if kind == "last":
                        layernorm()
                    rotate_next()
                pairs(pool, pair, seen)

            batches(pool, batch)

        @block.scalar
        def _(act):
            seen = Seen(act)

            def take_xt(g):
                for c in range(NC):
                    act.wait_ge(s_xt_act, seen(s_xt_act))
                    act.activation(xn_t[:, 0, c, :], ps_g[g.xt[c]][:, :], ACT.Copy).then_inc(s_xt_hi_dve, 1)

            def take_qkv(t, hp, g):
                gate = gate_cols(hp)
                ps = ps_g[g.qkv[t]][:, gate:]
                act.wait_ge(s_qkv_act, seen(s_qkv_act))
                act.activation(qk[:, t, :], ps[:, 0:2 * PW], ACT.Copy).then_inc(s_qk_dve, 1)
                if t >= 2:
                    act.wait_ge(s_sq_free, seen(s_sq_free))
                act.activation(qk_sq[:, t % 2, :], ps[:, 0:2 * PW], ACT.Square).then_inc(s_qk_dve, 1)
                if gate:
                    act.activation(scores_g[:, t, :], ps_g[g.qkv[t]][:, 0:E], ACT.Copy).then_inc(s_gate_dve, 1)
                act.activation(v[:, hp, t, :], ps[:, 2 * PW:3 * PW], ACT.Copy).then_inc(g_free[g.qkv[t]], 1)

            def take_qt(g):
                act.wait_ge(s_qt_act, seen(s_qt_act))
                act.activation(q_t[:, :], ps_g[g.qt][:, :], ACT.Copy).then_inc(g_free[g.qt], 1)

            def take_ot(hp, g):
                act.wait_ge(s_ot_act, seen(s_ot_act))
                act.activation(o_t[:, 0, hp, :], ps_g[g.ot][:, :], ACT.Copy).then_inc(s_ot_hi_dve, 1)

            def softmax(m):
                h, i = ITEMS[m]
                w = (i + 1) * P
                act.wait_ge(s_bias_act, seen(s_bias_act))
                act.activation(prob[:, m % 2, 0:w], ps_s[m % 2][:, 0:w], ACT.Exp, bias=bias[:, i, h:h + 1],
                               scale=q_scale[:, i, h:h + 1], accum_out=row_sum[:, i, h:h + 1]).then_inc(s_prob_pe, 1)

            def take_pt(m):
                w = (ITEMS[m][1] + 1) * P
                act.wait_ge(s_pt_act, seen(s_pt_act))
                act.activation(prob_t[:, m % 2, 0:w], ps_p[m % 2][:, 0:w], ACT.Copy).then_inc(s_prob_t_act, 1)

            take_xt(LAST_PAIR_BANKS)
            for t in range(NT):
                take_qkv(t, 0, LAST_PAIR_BANKS)
            take_qt(LAST_PAIR_BANKS)
            seen.settle()

            def batch(b, last):
                def pair(hp, kind, hp_prev, hp_next):
                    g, _, qkv_steps = plan(kind, last)
                    softmax(0)
                    for step in range(STEPS):
                        if step - 1 in BY_ACT:
                            take_pt(step - 1)
                        if step + 1 < NI:
                            softmax(step + 1)
                        if kind == "last" and not last and step == XT_STEP:
                            take_xt(g)
                        if step in qkv_steps:
                            take_qkv(qkv_steps[step], hp_next, g)
                        if kind != "first" and step == OT_STEP:
                            take_ot(hp_prev, g)
                    if kind == "last":
                        take_ot(hp, OWN_OT)
                    if not (kind == "last" and last):
                        take_qt(g)
                pairs(act, pair, seen)

            batches(act, batch)

        @block.tensor
        def _(pe):
            seen = Seen(pe)
            known_free = set()

            def bank(i):
                if i in known_free:
                    known_free.remove(i)
                else:
                    pe.wait_ge(g_free[i], seen(g_free[i]))
                return ps_g[i]

            def know_free(i):
                pe.wait_ge(g_free[i], seen(g_free[i]))
                known_free.add(i)

            def product(ps, lhs, rhs, parts=range(NC), last_part=NC - 1):
                for c in parts:
                    for a, b in TERMS:
                        r = pe.matmul(ps, lhs(a, c), rhs(b, c), start=(c == 0 and (a, b) == TERMS[0]),
                                      stop=(c == last_part and (a, b) == TERMS[-1]))
                return r

            def tile(t):
                return slice(t * P, (t + 1) * P)

            def transpose_xn(g):
                pe.wait_ge(s_xn_pe, seen(s_xn_pe))
                for c in range(NC):
                    ps = bank(g.xt[c])
                    for t in range(NT):
                        r = pe.transpose(ps[:, tile(t)], xn[:, t, tile(c)], ident[:, :])
                    r.then_inc(s_xt_act, 1)

            def qkv(t, hp, g):
                gate = gate_cols(hp)
                product(bank(g.qkv[t])[:, 0:gate + 3 * PW], lambda a, c: xn_t[:, a, c, tile(t)],
                        lambda b, c: w_qkv[:, b, c, bass.ds(hp * (3 * PW) + (E - gate), gate + 3 * PW)])\
                    .then_inc(s_qkv_act, 1)

            def expert(t, hp, g):
                product(bank(g.exp[t])[:, 0:C], lambda a, c: xn_t[:, a, c, tile(t)],
                        lambda b, c: w_exp[:, b, c, hp, :]).then_inc(s_expert_dve, 1)

            def transpose_o(g):
                pe.wait_ge(s_o_pe, seen(s_o_pe))
                ps = bank(g.ot)
                for t in range(NT):
                    r = pe.transpose(ps[:, tile(t)], o_rows[:, t, :], ident[:, :])
                r.then_inc(s_ot_act, 1)

            def project(t, ps, parts):
                return product(ps[:, (t % 2) * C:(t % 2 + 1) * C], lambda a, c: o_t[:, a, c, tile(t)],
                               lambda b, c: w_out[:, b, c, :], parts, PAIRS - 1)

            def output(g, last):
                ps = bank(g.proj[0])
                project(0, ps, range(0, PAIRS // 2))
                transpose_o(OWN_OT)
                project(0, ps, range(PAIRS // 2, PAIRS - 1))
                know_free(OWN_OT.ot)
                project(0, ps, range(PAIRS - 1, PAIRS))
                project(1, ps, range(PAIRS)).then_inc(s_proj_dve, 1)
                ps = ps_g[g.proj[1]]
                project(2, ps, range(PAIRS - 1, PAIRS))
                project(3, ps, range(0, PAIRS // 2))
                if not last:
                    transpose_qk(g)
                project(3, ps, range(PAIRS // 2, PAIRS)).then_inc(s_proj_dve, 1)

            def transpose_qk(g):
                pe.wait_ge(s_rot_pe, seen(s_rot_pe))
                for n, i, done in ((1, g.kt, s_kt_dve), (0, g.qt, s_qt_act)):
                    ps = bank(i)
                    for t in range(NT):
                        r = pe.transpose(ps[:, tile(t)], qk_rot[:, t, tile(n)], ident[:, :])
                    r.then_inc(done, 1)

            def scores(m):
                h, i = ITEMS[m]
                rows, w = slice(h * D, (h + 1) * D), (i + 1) * P
                ps = ps_s[m % 2]
                pe.matmul(ps[:, 0:w], q_t[rows, tile(i)], k_t[rows, 0:w], start=True, stop=True)
                pe.matmul(ps[:, tile(i)], ident_b[:, :], mask_b[:, :], start=False, stop=True,
                          skip_group_check=True).then_inc(s_scores_dve, 1)

            def transpose_probs(m):
                pe.wait_ge(s_prob_pe, seen(s_prob_pe))
                for j in range(ITEMS[m][1] + 1):
                    r = pe.transpose(ps_p[m % 2][:, tile(j)], prob[:, m % 2, tile(j)], ident[:, :])
                r.then_inc(s_pt_act if m in BY_ACT else s_pt_dve, 1)

            def values(m, hp):
                h, i = ITEMS[m]
                ready = s_prob_t_act if m in BY_ACT else s_prob_t_dve
                pe.wait_ge(ready, seen(ready))
                at = i * PW + h * D
                for j in range(i + 1):
                    r = pe.matmul(ps_o[:, at:at + D], prob_t[:, m % 2, tile(j)], v[:, hp, j, h * D:(h + 1) * D],
                                  start=(j == 0), stop=(j == i))
                return r

            for i in range(3):
                pe.sem_inc(g_free[i], 1)
            pe.wait_ge(s_masks_pe, seen(s_masks_pe))
            pe.wait_ge(s_weights_pe, seen(s_weights_pe))
            transpose_xn(LAST_PAIR_BANKS)
            for i in LAST_PAIR_BANKS.xt:
                know_free(i)
            for t in range(NT):
                qkv(t, 0, LAST_PAIR_BANKS)
            transpose_qk(LAST_PAIR_BANKS)
            seen.settle()

            def batch(b, last):
                def pair(hp, kind, hp_prev, hp_next):
                    g, expert_steps, qkv_steps = plan(kind, last)
                    for i in QK_BANKS:
                        know_free(i)
                    scores(0)
                    for step in range(STEPS):
                        if 1 <= step <= NI:
                            transpose_probs(step - 1)
                        if step + 1 < NI:
                            scores(step + 1)
                        if step in expert_steps:
                            expert(expert_steps[step], hp, g)
                        if kind == "last" and not last and step == XT_STEP:
                            transpose_xn(g)
                        if kind == "last" and step == PROJECT_STEP:
                            project(2, bank(g.proj[1]), range(PAIRS - 1))
                        if kind == "last" and not last and step == XT_STEP + 1:
                            for i in g.xt:
                                know_free(i)
                        if step in qkv_steps:
                            qkv(qkv_steps[step], hp_next, g)
                        if kind != "first" and step == OT_STEP:
                            transpose_o(g)
                        if step >= 2:
                            r = values(step - 2, hp)
                    r.then_inc(s_o_dve, 1)
                    if kind == "last":
                        output(g, last)
                    else:
                        transpose_qk(g)
                        expert(NT - 1, hp, g)
                pairs(pe, pair, seen)

            batches(pe, batch)

        @block.vector
        def _(dve):
            seen = Seen(dve)

            def own(r):
                r.then_inc(s_dve_self, 1)
                dve.wait_ge(s_dve_self, seen(s_dve_self))

            def row_stats(tiles):
                for t in tiles:
                    r = dve.bn_stats(ln_stat[:, t, :], xin[:, t, :])
                return r

            def variances(r):
                own(r)
                for t in range(NT):
                    r = dve.bn_aggr(ln_mv[:, t, :], ln_stat[:, t, :])
                own(r)
                dve.tensor_scalar(ln_ve[:, :], ln_mv[:, :, 1], LN_EPS, None, ALU.add).then_inc(s_var_pool, 1)

            def normalise_x():
                dve.wait_ge(s_rstd_dve, seen(s_rstd_dve))
                for t in range(NT):
                    r = dve.tensor_scalar(xn[:, t, :], xin[:, t, :], ln_mv[:, t, 0:1], ln_rstd[:, t:t + 1],
                                          ALU.subtract, ALU.mult)
                r.then_inc(s_xn_pe, 1)
                dve.drain().then_inc(s_xn_pool, 1)

            def take_xt(g):
                for c in range(NC):
                    dve.wait_ge(s_xt_hi_dve, seen(s_xt_hi_dve))
                    dve.tensor_tensor(xn_t[:, 1, c, :], ps_g[g.xt[c]][:, :], xn_t[:, 0, c, :].bitcast(F32), ALU.subtract)\
                        .then_inc(g_free[g.xt[c]], 1)

            def choose():
                dve.wait_ge(s_gate_dve, seen(s_gate_dve, NT))
                for t in range(NT):
                    r = dve.max(top[:, t, :], scores_g[:, t, :])
                own(r)
                for t in range(NT):
                    r = dve.max_index(top_i[:, t, :], top[:, t, :], scores_g[:, t, :])
                own(r)
                own(dve.tensor_copy(chosen[:, :], top_i[:, :, 0]))
                for t in range(NT):
                    r = dve.tensor_scalar(onehot[:, t, :], expert_no[:, :], chosen[:, t:t + 1], None, ALU.is_equal)
                own(r)

            def rope_products(t):
                dve.wait_ge(s_qk_dve, seen(s_qk_dve))
                src = qk[:, t, :].rearrange("p (n h d) -> p n h d", n=2, h=2)
                for dst, table in ((qk_cos, t_cos), (qk_sin, t_sin)):
                    r = dve.tensor_tensor(dst[:, t, :].rearrange("p (n h d) -> p n h d", n=2, h=2), src,
                                          table[:, t, :, :].unsqueeze(2).to_broadcast([P, 2, 2, D]), ALU.mult)
                r.then_inc(s_products_pool, 1)
                dve.wait_ge(s_qk_dve, seen(s_qk_dve))
                r = dve.tensor_reduce(ss[:, t, :], qk_sq[:, t % 2, :].rearrange("p (n d) -> p n d", d=D), AX.X, ALU.add)
                if t < 2:
                    r.then_inc(s_sq_free, 1)
                if t == NT - 1:
                    own(r)
                    dve.tensor_scalar(ms[:, :, :], ss[:, :, :], 1.0 / D, RMS_EPS, ALU.mult, ALU.add).then_inc(s_ms_pool, 1)

            def take_kt(g):
                dve.wait_ge(s_kt_dve, seen(s_kt_dve))
                dve.tensor_scalar(q_scale[:, :, :], rms_inv[:, :, 0:2], SCALE, None, ALU.mult)
                dve.tensor_copy(k_t[:, :], ps_g[g.kt][:, :]).then_inc(g_free[g.kt], 1)

            def row_max(m):
                h, i = ITEMS[m]
                dve.wait_ge(s_scores_dve, seen(s_scores_dve))
                own(dve.tensor_reduce(neg_max[:, i, h:h + 1], ps_s[m % 2][:, 0:(i + 1) * P], AX.X, ALU.max, negate=True))
                dve.tensor_tensor(bias[:, i, h:h + 1], neg_max[:, i, h:h + 1], q_scale[:, i, h:h + 1], ALU.mult)\
                    .then_inc(s_bias_act, 1)

            def take_pt(m):
                w = (ITEMS[m][1] + 1) * P
                dve.wait_ge(s_pt_dve, seen(s_pt_dve))
                dve.tensor_copy(prob_t[:, m % 2, 0:w], ps_p[m % 2][:, 0:w]).then_inc(s_prob_t_dve, 1)

            def take_ot(hp, g):
                dve.wait_ge(s_ot_hi_dve, seen(s_ot_hi_dve))
                dve.tensor_tensor(o_t[:, 1, hp, :], ps_g[g.ot][:, :], o_t[:, 0, hp, :].bitcast(F32), ALU.subtract)\
                    .then_inc(g_free[g.ot], 1)

            def take_expert(t, hp, first, g):
                dve.wait_ge(s_expert_dve, seen(s_expert_dve))
                dve.scalar_tensor_tensor(acc[:, t, :], ps_g[g.exp[t]][:, 0:C], onehot[:, t, bass.ds(hp, 1)],
                                         res[:, t, :] if first else acc[:, t, :], ALU.mult, ALU.add)\
                    .then_inc(g_free[g.exp[t]], 1)

            def invert_sums():
                dve.wait_ge(s_o_dve, seen(s_o_dve))
                own(dve.reciprocal(row_inv[:, :, :], row_sum[:, :, :]))

            def normalise():
                dve.tensor_tensor(o_rows[:, :, :].rearrange("p t (h d) -> p (t h) d", d=D),
                                  ps_o[:, :].rearrange("p (n d) -> p n d", d=D),
                                  row_inv[:, :, :].rearrange("p t h -> p (t h)").unsqueeze(2).to_broadcast([P, NI, D]),
                                  ALU.mult).then_inc(s_o_pe, 1)

            def output(last, g):
                if last:
                    dve.wait_ge(s_out_stored, seen(s_out_stored, 16))
                else:
                    dve.wait_ge(s_res_dve, seen(s_res_dve))
                for half in range(2):
                    dve.wait_ge(s_proj_dve, seen(s_proj_dve))
                    rows = slice(2 * half, 2 * half + 2)
                    dve.tensor_tensor(out_sb[:, rows, :], ps_g[g.proj[half]][:, :].rearrange("p (t c) -> p t c", c=C),
                                      acc[:, rows, :], ALU.add).then_inc(g_free[g.proj[half]], 1)
                    if half == 0 and not last:
                        take_kt(g)
                dve.drain().then_inc(s_out_ready, 1)
                if not last:
                    dve.drain().then_inc(s_x_free, 1)

            dve.wait_ge(s_consts_dve, seen(s_consts_dve, 64))
            variances(row_stats(range(NT)))
            normalise_x()
            for table in (t_cos, t_sin):
                own(dve.tensor_copy(table[:, :, 1, :], table[:, :, 0, :]))
                for t in range(NT):
                    dve.tensor_tensor(table[:, t, :, :], table[:, t, :, :], nw[:, :, :], ALU.mult)
            for n, (dst, src) in enumerate(weight_chunks()):
                dve.wait_ge(w_loaded[n % 2], seen(w_loaded[n % 2], 16))
                w = staged[:, (n % 2) * chunk:(n % 2) * chunk + src.free_size()]
                own(dve.tensor_copy(dst[:, 0, :], w))
                dve.tensor_tensor(dst[:, 1, :], w, dst[:, 0, :].bitcast(F32), ALU.subtract).then_inc(s_w_free, 1)
            dve.drain().then_inc(s_weights_pe, 1)
            take_xt(LAST_PAIR_BANKS)
            for t in range(NT):
                rope_products(t)
            take_kt(LAST_PAIR_BANKS)
            dve.wait_ge(s_iota_dve, seen(s_iota_dve))
            choose()
            dve.wait_ge(s_res_dve, seen(s_res_dve))
            dve.drain().then_inc(s_x_free, 1)
            row_max(0)
            seen.settle()

            def batch(b, last):
                def pair(hp, kind, hp_prev, hp_next):
                    g, expert_steps, qkv_steps = plan(kind, last)
                    if kind == "last" and not last:
                        dve.wait_ge(s_x_loaded, seen(s_x_loaded, 16))
                    for step in range(STEPS):
                        m = step - 1
                        if 0 <= m < NI and m not in BY_ACT:
                            take_pt(m)
                        if step + 1 < NI:
                            row_max(step + 1)
                        if step - 1 in qkv_steps:
                            rope_products(qkv_steps[step - 1])
                        if step in expert_steps:
                            take_expert(expert_steps[step], hp, kind == "first", g)
                        if kind == "last" and not last:
                            if step in STATS_STEPS:
                                r = row_stats(STATS_STEPS[step])
                            if step == max(STATS_STEPS):
                                variances(r)
                            if step == NORM_STEP:
                                dve.wait_ge(s_out_stored, seen(s_out_stored, 16))
                                normalise_x()
                            if step == XT_STEP:
                                take_xt(g)
                        if kind != "first" and step == OT_STEP:
                            take_ot(hp_prev, g)
                    if kind == "last":
                        invert_sums()
                        normalise()
                        if not last:
                            choose()
                        take_ot(hp, OWN_OT)
                        output(last, g)
                        if not last:
                            row_max(0)
                    else:
                        take_kt(g)
                        invert_sums()
                        row_max(0)
                        normalise()
                        take_expert(NT - 1, hp, kind == "first", g)
                pairs(dve, pair, seen)

            batches(dve, batch)


def rope_tables(T, half):
    f = np.float32
    expo = (np.arange(0, 2 * half, 2, dtype=f) / f(2 * half)).astype(np.float64)
    inv = (1.0 / (10000.0 ** expo).astype(f).astype(np.float64)).astype(f)
    ang = (np.arange(T, dtype=f)[:, None] * inv).astype(np.float64)
    return np.cos(ang).astype(f), np.sin(ang).astype(f)


def kernel(**inputs):
    import concourse.bacc as bacc
    from concourse.bass_utils import run_bass_kernel_spmd

    x = np.ascontiguousarray(inputs["L0_attn_x"])
    B, T, C = x.shape
    nt, ncp = T // P, C // P
    wqkv = np.asarray(inputs["L0_attn_wqkv"])
    wqkv_t = wqkv.reshape(3, PAIRS, 2 * D, ncp, P).transpose(4, 3, 1, 0, 2).reshape(P, ncp, PAIRS * 6 * D)
    wo_t = np.asarray(inputs["L0_attn_wo"]).reshape(C, PAIRS, 2 * D).transpose(2, 1, 0)
    gate_w = np.asarray(inputs["L0_ffn_gate_w"])
    gate_t = gate_w.reshape(-1, ncp, P).transpose(2, 1, 0)
    wqkv_t = np.concatenate([gate_t, wqkv_t], axis=2)
    expert_t = np.asarray(inputs["L0_ffn_expert_w"]).reshape(-1, C, ncp, P).transpose(3, 2, 0, 1)
    norm_w = np.stack([np.asarray(inputs["L0_attn_q_norm_w"]), np.asarray(inputs["L0_attn_k_norm_w"])])
    norm_w = np.broadcast_to(norm_w, (P, 2, D))
    cos, sin = rope_tables(T, D // 2)
    rope_cos = np.concatenate([cos, cos], 1).reshape(nt, P, D).transpose(1, 0, 2)
    rope_sin = np.concatenate([sin, -sin], 1).reshape(nt, P, D).transpose(1, 0, 2)

    arrays = {
        "x": x, "wqkv_t": wqkv_t, "wo_t": wo_t, "norm_w": norm_w, "rope_cos": rope_cos, "rope_sin": rope_sin,
        "expert_t": expert_t,
    }
    arrays = {f"in_{k}": np.ascontiguousarray(a) for k, a in arrays.items()}
    nc = bacc.Bacc("TRN2", target_bir_lowering=False, num_devices=1)
    args = [nc.dram_tensor(k, a.shape, mybir.dt.from_np(a.dtype), kind="ExternalInput").ap() for k, a in arrays.items()]
    args.append(nc.dram_tensor("out", x.shape, F32, kind="ExternalOutput").ap())
    block_program(nc, *args)
    r = run_bass_kernel_spmd(nc, [arrays], core_ids=[0])
    return r.results[0]["out"]
```

```python
from contextlib import ExitStack

import numpy as np

import concourse.bass as bass
from concourse import mybir
from concourse.alu_op_type import AluOpType as ALU

ACT = mybir.ActivationFunctionType
AX = mybir.AxisListType
F32 = mybir.dt.float32
F32R = mybir.dt.float32r
BF16 = mybir.dt.bfloat16
U32 = mybir.dt.uint32

P = 128
HEADS = 16
D = 64
HEADS_OF_PAIR = 2
PAIRS = HEADS // HEADS_OF_PAIR
SCALE = D ** -0.5
RMS_EPS = 1e-6
LN_EPS = 1e-5
MASKED = -1e30
TERMS = ((0, 0), (0, 1), (1, 0))


class Banks:

    def __init__(self, qkv, qt=None, kt=None, ot=None, proj=None, exp=None, xt=None):
        self.qkv, self.qt, self.kt, self.ot = qkv, qt, kt, ot
        self.proj, self.exp, self.xt = proj, exp, xt


PAIR_BANKS = Banks(qkv=(2, 1, 0, 1), ot=2, exp=(0, 2, 1, 0), qt=2, kt=0)
LAST_PAIR_BANKS = Banks(exp=(2, 1, 0, 1), ot=2, xt=(0, 2), qkv=(0, 2, 0, 2), proj=(0, 1), qt=2, kt=0)
OWN_OT = Banks(qkv=None, ot=2)
QKV_STEPS = {0: 0, 1: 1, 2: 2, 3: 3}
EXPERT_STEPS = {4: 0, 5: 1, 8: 2}
LAST_EXPERT_STEPS = {0: 0, 1: 1, 2: 2, 3: 3}
XT_STEP = 4
QK_STEP = 8
CHOOSE_STEP = 2
PROJECT_STEP = 5
LAST_QKV_STEPS = {5: 0, 6: 1, 7: 2, 8: 3}
STATS_STEPS = {0: (0, 1), 1: (2, 3)}
NORM_STEP = 2
OT_STEP = 2
ITEMS = [(h, i) for i in (1, 3, 2, 0) for h in range(2)]
STEPS = len(ITEMS) + 2
BY_ACT = (0, 2, 3, 4, 6)


class Seen:

    def __init__(self, eng):
        self.eng, self.n = eng, {}

    def __call__(self, sem, by=1):
        self.n[sem] = self.n.get(sem, 0) + by
        return self.n[sem]

    def settle(self):
        for sem, n in self.n.items():
            self.eng.sem_inc(sem, -n)
        self.n = {}


def block_program(nc, x, wqkv_t, wo_t, norm_w, rope_cos, rope_sin, expert_t, out):
    B, T, C = x.shape
    NT = T // P
    NC = C // P
    E = expert_t.shape[2]
    NI = HEADS_OF_PAIR * NT
    PW = 2 * D
    assert PW == P and E == PAIRS and C == 2 * P and T == 512

    x_rows = x.rearrange("b (t p) c -> b p t c", p=P)
    out_rows = out.rearrange("b (t p) c -> b p t c", p=P)

    with ExitStack() as ctx:
        def sb(name, shape, dt=F32):
            return ctx.enter_context(nc.sbuf_tensor(name, shape, dt))

        def sem(name):
            return ctx.enter_context(nc.semaphore(name))

        w_qkv = sb("w_qkv", [P, 2, NC, E + PAIRS * 3 * PW], F32R)
        w_exp = sb("w_exp", [P, 2, NC, E, C], F32R)
        w_out = sb("w_out", [P, 2, PAIRS, C], F32R)
        t_cos = sb("t_cos", [P, NT, 2, D])
        t_sin = sb("t_sin", [P, NT, 2, D])
        nw = sb("nw", [P, 2, D])
        ident = sb("ident", [P, P])
        ident_b = sb("ident_b", [P, P], BF16)
        mask_b = sb("mask_b", [P, P], BF16)
        expert_no = sb("expert_no", [P, E])
        expert_no_i = sb("expert_no_i", [P, E], mybir.dt.int32)
        neg_half = sb("neg_half", [P, NT])

        xin = sb("xin", [P, NT, C])
        xn = sb("xn", [P, NT, C])
        out_sb = xn
        res = sb("res", [P, NT, C])
        acc = sb("acc", [P, NT, C])
        xn_t = sb("xn_t", [P, 2, NC, T], F32R)
        o_t = sb("o_t", [P, 2, PAIRS, T], F32R)
        ln_stat = sb("ln_stat", [P, NT, 6])
        ln_mv = sb("ln_mv", [P, NT, 2])
        ln_ve = sb("ln_ve", [P, NT])
        ln_rstd = sb("ln_rstd", [P, NT])
        top = sb("top", [P, NT, 8])
        top_i = sb("top_i", [P, NT, 8], U32)
        chosen = sb("chosen", [P, NT])
        onehot = sb("onehot", [P, NT, E])
        scores_g = sb("scores_g", [P, NT, E])

        work = sb("work", [P, 4, NT * 2 * PW])
        qk = work[:, 0, :].rearrange("p (t n) -> p t n", t=NT)
        qk_cos = work[:, 1, :].rearrange("p (t n) -> p t n", t=NT)
        qk_sin = work[:, 2, :].rearrange("p (t n) -> p t n", t=NT)
        qk_rot = work[:, 3, :].rearrange("p (t n) -> p t n", t=NT)
        qk_sq = sb("qk_sq", [P, 2, 4, D + 1])
        v = sb("v", [P, 2, NT, PW])
        ss = sb("ss", [P, NT, 4])
        rms_inv = sb("rms_inv", [P, NT, 4])
        q_scale = sb("q_scale", [P, NT, 2])
        q_t = sb("q_t", [P, 2, T], F32R)
        k_t = sb("k_t", [P, 2, T], F32R)
        prob = sb("prob", [P, 2, T])
        prob_t = sb("prob_t", [P, 2, T])
        neg_max = sb("neg_max", [P, NT, 2])
        bias = sb("bias", [P, NT, 2])
        row_sum = sb("row_sum", [P, NT, 2])
        row_inv = sb("row_inv", [P, NT, 2])
        o_rows = sb("o_rows", [P, NT, PW])

        ps_g = [ctx.enter_context(nc.psum_tensor(f"ps_g{i}", [P, 512], F32)) for i in range(3)]
        ps_s = [ctx.enter_context(nc.psum_tensor(f"ps_s{i}", [P, 512], F32)) for i in range(2)]
        ps_p = [ctx.enter_context(nc.psum_tensor(f"ps_p{i}", [P, 512], F32)) for i in range(2)]
        ps_o = ctx.enter_context(nc.psum_tensor("ps_o", [P, 512], F32))

        s_consts_dve = sem("s_consts_dve")
        s_iota_dve = sem("s_iota_dve")
        s_pool_self = sem("s_pool_self")
        s_masks_pe = sem("s_masks_pe")
        s_weights_pe = sem("s_weights_pe")
        w_loaded = [sem(f"w_loaded{i}") for i in range(2)]
        s_w_free = sem("s_w_free")
        s_x_loaded = sem("s_x_loaded")
        s_x_free = sem("s_x_free")
        s_var_pool = sem("s_var_pool")
        s_rstd_dve = sem("s_rstd_dve")
        s_xn_pe = sem("s_xn_pe")
        s_xn_pool = sem("s_xn_pool")
        s_res_dve = sem("s_res_dve")
        s_xt_act = sem("s_xt_act")
        s_xt_hi_dve = sem("s_xt_hi_dve")
        s_gate_dve = sem("s_gate_dve")
        s_qkv_act = sem("s_qkv_act")
        s_qk_dve = sem("s_qk_dve")
        s_sq_free = sem("s_sq_free")
        s_products_pool = sem("s_products_pool")
        s_ss_pool = sem("s_ss_pool")
        s_rot_pe = sem("s_rot_pe")
        s_qk_t_act = sem("s_qk_t_act")
        s_qk_hi_dve = sem("s_qk_hi_dve")
        s_scores_dve = sem("s_scores_dve")
        s_bias_act = sem("s_bias_act")
        s_prob_pe = sem("s_prob_pe")
        s_pt_act = sem("s_pt_act")
        s_pt_dve = sem("s_pt_dve")
        s_prob_t_act = sem("s_prob_t_act")
        s_prob_t_dve = sem("s_prob_t_dve")
        s_expert_dve = sem("s_expert_dve")
        s_o_dve = sem("s_o_dve")
        s_o_pe = sem("s_o_pe")
        s_ot_act = sem("s_ot_act")
        s_ot_hi_dve = sem("s_ot_hi_dve")
        s_proj_dve = sem("s_proj_dve")
        s_dve_self = sem("s_dve_self")
        s_out_ready = sem("s_out_ready")
        s_out_stored = sem("s_out_stored")
        s_out_last = sem("s_out_last")
        g_free = [sem(f"g_free{i}") for i in range(3)]

        block = ctx.enter_context(nc.Block())

        def batches(eng, batch):
            with eng.Fori(0, B - 1) as b:
                batch(b, False)
            batch(B - 1, True)

        def pairs(eng, pair, seen):
            pair(0, "first", PAIRS - 1, 1, 0)
            seen.settle()
            with eng.Fori(0, PAIRS // 2 - 1) as n:
                pair(n * 2 + 1, "inner", n * 2, n * 2 + 2, 1)
                pair(n * 2 + 2, "inner", n * 2 + 1, n * 2 + 3, 0)
                seen.settle()
            pair(PAIRS - 1, "last", PAIRS - 2, 0, 1)
            seen.settle()

        def gate_cols(hp):
            return E if isinstance(hp, int) and hp == 0 else 0

        def plan(kind, last):
            if kind != "last":
                return PAIR_BANKS, EXPERT_STEPS, QKV_STEPS
            return LAST_PAIR_BANKS, LAST_EXPERT_STEPS, {} if last else LAST_QKV_STEPS

        chunk = 2 * P * NT * 2
        staged = work[:, :, :].rearrange("p a n -> p (a n)")

        def weight_chunks():
            cols = PAIRS * 3 * PW // 2
            for c in range(NC):
                for at, n in ((0, E + cols), (E + cols, cols)):
                    yield w_qkv[:, :, c, at:at + n], wqkv_t[:, c, at:at + n]
            for c in range(NC):
                yield (w_exp[:, :, c, :, :].rearrange("p a e n -> p a (e n)"),
                       expert_t[:, c, :, :].rearrange("p e n -> p (e n)"))
            yield (w_out[:, :, :, :].rearrange("p a h n -> p a (h n)"), wo_t.rearrange("p h n -> p (h n)"))

        @block.sync
        def _(sp):
            seen = Seen(sp)
            for dst, src in ((xin[:, :, :], x_rows[0]), (nw[:, :, :], norm_w), (t_cos[:, :, 0, :], rope_cos),
                             (t_sin[:, :, 0, :], rope_sin)):
                sp.dma_start(dst, src).then_inc(s_consts_dve, 16)
            for n, (dst, src) in enumerate(weight_chunks()):
                if n >= 2:
                    sp.wait_ge(s_w_free, seen(s_w_free))
                at = (n % 2) * chunk
                sp.dma_start(staged[:, at:at + src.free_size()], src).then_inc(w_loaded[n % 2], 16)
            sp.sem_inc(s_out_stored, 16)
            seen.settle()

            def batch(b, last):
                if not last:
                    sp.wait_ge(s_x_free, seen(s_x_free))
                    sp.dma_start(xin[:, :, :], x_rows[b + 1]).then_inc(s_x_loaded, 16)
                sp.wait_ge(s_out_ready, seen(s_out_ready))
                sp.dma_start(out_rows[b], out_sb[:, :, :]).then_inc(s_out_last if last else s_out_stored, 16)
                seen.settle()

            batches(sp, batch)
            sp.wait_ge(s_out_last, 16)

        @block.gpsimd
        def _(pool):
            seen = Seen(pool)
            pool.memset(ident[:, :], 0.0)
            pool.memset(ident_b[:, :], 0.0)
            pool.memset(mask_b[:, :], 0.0)
            pool.memset(neg_half[:, :], -0.5)
            pool.memset(qk_sq[:, :, :, D:D + 1], D * RMS_EPS)
            pool.iota(expert_no_i[:, :], [[1, E]], base=0, channel_multiplier=0).then_inc(s_pool_self, 1)
            pool.wait_ge(s_pool_self, seen(s_pool_self))
            for m in (ident, ident_b):
                pool.affine_select(out=m[:, :], in_=m[:, :], compare_op=ALU.not_equal, fill=1.0,
                                   base=0, pattern=[[-1, P]], channel_multiplier=1)
            pool.affine_select(out=mask_b[:, :], in_=mask_b[:, :], compare_op=ALU.is_ge, fill=MASKED,
                               base=0, pattern=[[-1, P]], channel_multiplier=1).then_inc(s_masks_pe, 1)
            pool.tensor_copy(expert_no[:, :], expert_no_i[:, :]).then_inc(s_iota_dve, 1)

            def layernorm():
                pool.wait_ge(s_var_pool, seen(s_var_pool))
                pool.tensor_tensor(ln_rstd[:, :], ln_ve[:, :], neg_half[:, :], ALU.pow).then_inc(s_rstd_dve, 1)
                pool.wait_ge(s_xn_pool, seen(s_xn_pool))
                pool.tensor_tensor(res[:, :, :], xin[:, :, :], xn[:, :, :], ALU.add).then_inc(s_res_dve, 1)

            def rotate_next():
                for t in range(NT):
                    cos, sin, rot = [y[:, t, :].rearrange("p (h two d) -> p h two d", two=2, d=D // 2)
                                     for y in (qk_cos, qk_sin, qk_rot)]
                    pool.wait_ge(s_products_pool, seen(s_products_pool))
                    for a in range(2):
                        pool.tensor_tensor(rot[:, :, a, :], cos[:, :, a, :], sin[:, :, 1 - a, :], ALU.add)
                    pool.wait_ge(s_ss_pool, seen(s_ss_pool))
                    pool.tensor_tensor(rms_inv[:, t, :], ss[:, t, :], neg_half[:, :], ALU.pow)\
                        .then_inc(s_pool_self, 1)
                    pool.wait_ge(s_pool_self, seen(s_pool_self))
                    k_rot = qk_rot[:, t, PW:].rearrange("p (h d) -> p h d", d=D)
                    r = pool.tensor_tensor(k_rot, k_rot, rms_inv[:, t, 2:4].unsqueeze(2).to_broadcast([P, 2, D]), ALU.mult)
                r.then_inc(s_rot_pe, 1)

            layernorm()
            rotate_next()
            seen.settle()

            def batch(b, last):
                def pair(hp, kind, hp_prev, hp_next, slot):
                    if kind == "last" and last:
                        return
                    if kind == "last":
                        layernorm()
                    rotate_next()
                pairs(pool, pair, seen)

            batches(pool, batch)

        @block.scalar
        def _(act):
            seen = Seen(act)

            def take_xt(g):
                for c in range(NC):
                    act.wait_ge(s_xt_act, seen(s_xt_act))
                    act.activation(xn_t[:, 0, c, :], ps_g[g.xt[c]][:, :], ACT.Copy).then_inc(s_xt_hi_dve, 1)

            def take_qkv(t, hp, slot, g):
                gate = gate_cols(hp)
                ps = ps_g[g.qkv[t]][:, gate:]
                act.wait_ge(s_qkv_act, seen(s_qkv_act))
                act.activation(qk[:, t, :], ps[:, 0:2 * PW], ACT.Copy).then_inc(s_qk_dve, 1)
                if t >= 2:
                    act.wait_ge(s_sq_free, seen(s_sq_free))
                act.activation(qk_sq[:, t % 2, :, 0:D], ps[:, 0:2 * PW].rearrange("p (n d) -> p n d", d=D), ACT.Square).then_inc(s_qk_dve, 1)
                if gate:
                    act.activation(scores_g[:, t, :], ps_g[g.qkv[t]][:, 0:E], ACT.Copy).then_inc(s_gate_dve, 1)
                act.activation(v[:, slot, t, :], ps[:, 2 * PW:3 * PW], ACT.Copy).then_inc(g_free[g.qkv[t]], 1)

            def take_qk(g):
                for dst, i in ((k_t, g.kt), (q_t, g.qt)):
                    act.wait_ge(s_qk_t_act, seen(s_qk_t_act))
                    act.activation(dst[:, 0, :], ps_g[i][:, :], ACT.Copy).then_inc(s_qk_hi_dve, 1)

            def take_ot(hp, g):
                act.wait_ge(s_ot_act, seen(s_ot_act))
                act.activation(o_t[:, 0, hp, :], ps_g[g.ot][:, :], ACT.Copy).then_inc(s_ot_hi_dve, 1)

            def softmax(m):
                h, i = ITEMS[m]
                w = (i + 1) * P
                act.wait_ge(s_bias_act, seen(s_bias_act))
                act.activation(prob[:, m % 2, 0:w], ps_s[m % 2][:, 0:w], ACT.Exp, bias=bias[:, i, h:h + 1],
                               scale=q_scale[:, i, h:h + 1], accum_out=row_sum[:, i, h:h + 1]).then_inc(s_prob_pe, 1)

            def take_pt(m):
                w = (ITEMS[m][1] + 1) * P
                act.wait_ge(s_pt_act, seen(s_pt_act))
                act.activation(prob_t[:, m % 2, 0:w], ps_p[m % 2][:, 0:w], ACT.Copy).then_inc(s_prob_t_act, 1)

            take_xt(LAST_PAIR_BANKS)
            for t in range(NT):
                take_qkv(t, 0, 0, LAST_PAIR_BANKS)
            take_qk(LAST_PAIR_BANKS)
            seen.settle()

            def batch(b, last):
                def pair(hp, kind, hp_prev, hp_next, slot):
                    g, _, qkv_steps = plan(kind, last)
                    softmax(0)
                    for step in range(STEPS):
                        if step - 1 in BY_ACT:
                            take_pt(step - 1)
                        if step + 1 < NI:
                            softmax(step + 1)
                        if kind == "last" and not last and step == XT_STEP:
                            take_xt(g)
                        if step in qkv_steps:
                            take_qkv(qkv_steps[step], hp_next, 1 - slot, g)
                        if kind != "first" and step == OT_STEP:
                            take_ot(hp_prev, g)
                        if kind != "last" and step == QK_STEP:
                            take_qk(g)
                    if kind == "last":
                        take_ot(hp, OWN_OT)
                        if not last:
                            take_qk(g)
                pairs(act, pair, seen)

            batches(act, batch)

        @block.tensor
        def _(pe):
            seen = Seen(pe)
            known_free = set()

            def bank(i):
                if i in known_free:
                    known_free.remove(i)
                else:
                    pe.wait_ge(g_free[i], seen(g_free[i]))
                return ps_g[i]

            def know_free(i):
                pe.wait_ge(g_free[i], seen(g_free[i]))
                known_free.add(i)

            def product(ps, lhs, rhs, parts=range(NC), last_part=NC - 1):
                for c in parts:
                    for a, b in TERMS:
                        r = pe.matmul(ps, lhs(a, c), rhs(b, c), start=(c == 0 and (a, b) == TERMS[0]),
                                      stop=(c == last_part and (a, b) == TERMS[-1]))
                return r

            def tile(t):
                return slice(t * P, (t + 1) * P)

            def transpose_xn(g):
                pe.wait_ge(s_xn_pe, seen(s_xn_pe))
                for c in range(NC):
                    ps = bank(g.xt[c])
                    for t in range(NT):
                        r = pe.transpose(ps[:, tile(t)], xn[:, t, tile(c)], ident[:, :])
                    r.then_inc(s_xt_act, 1)

            def qkv(t, hp, g):
                gate = gate_cols(hp)
                product(bank(g.qkv[t])[:, 0:gate + 3 * PW], lambda a, c: xn_t[:, a, c, tile(t)],
                        lambda b, c: w_qkv[:, b, c, bass.ds(hp * (3 * PW) + (E - gate), gate + 3 * PW)])\
                    .then_inc(s_qkv_act, 1)

            def expert(t, hp, g):
                product(bank(g.exp[t])[:, 0:C], lambda a, c: xn_t[:, a, c, tile(t)],
                        lambda b, c: w_exp[:, b, c, hp, :]).then_inc(s_expert_dve, 1)

            def transpose_o(g):
                pe.wait_ge(s_o_pe, seen(s_o_pe))
                ps = bank(g.ot)
                for t in range(NT):
                    r = pe.transpose(ps[:, tile(t)], o_rows[:, t, :], ident[:, :])
                r.then_inc(s_ot_act, 1)

            def project(t, ps, parts):
                return product(ps[:, (t % 2) * C:(t % 2 + 1) * C], lambda a, c: o_t[:, a, c, tile(t)],
                               lambda b, c: w_out[:, b, c, :], parts, PAIRS - 1)

            def output(g, last):
                ps = bank(g.proj[0])
                project(0, ps, range(0, PAIRS // 2))
                transpose_o(OWN_OT)
                project(0, ps, range(PAIRS // 2, PAIRS - 1))
                know_free(OWN_OT.ot)
                project(0, ps, range(PAIRS - 1, PAIRS))
                project(1, ps, range(PAIRS)).then_inc(s_proj_dve, 1)
                ps = ps_g[g.proj[1]]
                project(2, ps, range(PAIRS - 1, PAIRS))
                project(3, ps, range(0, PAIRS // 2))
                if not last:
                    transpose_qk(g)
                project(3, ps, range(PAIRS // 2, PAIRS)).then_inc(s_proj_dve, 1)

            def transpose_qk(g):
                pe.wait_ge(s_rot_pe, seen(s_rot_pe))
                for n, i in ((1, g.kt), (0, g.qt)):
                    ps = bank(i)
                    for t in range(NT):
                        r = pe.transpose(ps[:, tile(t)], qk_rot[:, t, tile(n)], ident[:, :])
                    r.then_inc(s_qk_t_act, 1)

            def scores(m):
                h, i = ITEMS[m]
                rows, w = slice(h * D, (h + 1) * D), (i + 1) * P
                ps = ps_s[m % 2]
                for n, (a, b) in enumerate(TERMS):
                    pe.matmul(ps[:, 0:w], q_t[rows, a, tile(i)], k_t[rows, b, 0:w], start=(n == 0), stop=(n == 2))
                pe.matmul(ps[:, tile(i)], ident_b[:, :], mask_b[:, :], start=False, stop=True,
                          skip_group_check=True).then_inc(s_scores_dve, 1)

            def transpose_probs(m):
                pe.wait_ge(s_prob_pe, seen(s_prob_pe))
                for j in range(ITEMS[m][1] + 1):
                    r = pe.transpose(ps_p[m % 2][:, tile(j)], prob[:, m % 2, tile(j)], ident[:, :])
                r.then_inc(s_pt_act if m in BY_ACT else s_pt_dve, 1)

            def values(m, slot):
                h, i = ITEMS[m]
                ready = s_prob_t_act if m in BY_ACT else s_prob_t_dve
                pe.wait_ge(ready, seen(ready))
                at = i * PW + h * D
                for j in range(i + 1):
                    r = pe.matmul(ps_o[:, at:at + D], prob_t[:, m % 2, tile(j)], v[:, slot, j, h * D:(h + 1) * D],
                                  start=(j == 0), stop=(j == i))
                return r

            for i in range(3):
                pe.sem_inc(g_free[i], 1)
            pe.wait_ge(s_masks_pe, seen(s_masks_pe))
            pe.wait_ge(s_weights_pe, seen(s_weights_pe))
            transpose_xn(LAST_PAIR_BANKS)
            for i in LAST_PAIR_BANKS.xt:
                know_free(i)
            for t in range(NT):
                qkv(t, 0, LAST_PAIR_BANKS)
            transpose_qk(LAST_PAIR_BANKS)
            seen.settle()

            def batch(b, last):
                def pair(hp, kind, hp_prev, hp_next, slot):
                    g, expert_steps, qkv_steps = plan(kind, last)
                    known_free.clear()
                    know_free(g.qt)
                    if kind == "first":
                        know_free(g.kt)
                    scores(0)
                    for step in range(STEPS):
                        if kind != "last" and step == QK_STEP:
                            transpose_qk(g)
                        if 1 <= step <= NI:
                            transpose_probs(step - 1)
                        if step + 1 < NI:
                            scores(step + 1)
                        if step in expert_steps:
                            expert(expert_steps[step], hp, g)
                        if kind == "last" and step == PROJECT_STEP:
                            project(2, bank(g.proj[1]), range(PAIRS - 1))
                        if kind == "last" and not last and step == XT_STEP + 1:
                            for i in g.xt:
                                know_free(i)
                        if step in qkv_steps:
                            qkv(qkv_steps[step], hp_next, g)
                        if kind != "first" and step == OT_STEP:
                            transpose_o(g)
                        if step >= 2:
                            r = values(step - 2, slot)
                        if kind == "last" and not last and step == XT_STEP:
                            transpose_xn(g)
                    r.then_inc(s_o_dve, 1)
                    if kind == "last":
                        output(g, last)
                    else:
                        expert(NT - 1, hp, g)
                pairs(pe, pair, seen)

            batches(pe, batch)

        @block.vector
        def _(dve):
            seen = Seen(dve)

            def own(r):
                r.then_inc(s_dve_self, 1)
                dve.wait_ge(s_dve_self, seen(s_dve_self))

            def row_stats(tiles):
                for t in tiles:
                    r = dve.bn_stats(ln_stat[:, t, :], xin[:, t, :])
                return r

            def variances(r):
                own(r)
                for t in range(NT):
                    r = dve.bn_aggr(ln_mv[:, t, :], ln_stat[:, t, :])
                own(r)
                dve.tensor_scalar(ln_ve[:, :], ln_mv[:, :, 1], LN_EPS, None, ALU.add).then_inc(s_var_pool, 1)

            def normalise_x():
                dve.wait_ge(s_rstd_dve, seen(s_rstd_dve))
                for t in range(NT):
                    r = dve.tensor_scalar(xn[:, t, :], xin[:, t, :], ln_mv[:, t, 0:1], ln_rstd[:, t:t + 1],
                                          ALU.subtract, ALU.mult)
                r.then_inc(s_xn_pe, 1)
                dve.drain().then_inc(s_xn_pool, 1)

            def take_xt(g):
                for c in range(NC):
                    dve.wait_ge(s_xt_hi_dve, seen(s_xt_hi_dve))
                    dve.tensor_tensor(xn_t[:, 1, c, :], ps_g[g.xt[c]][:, :], xn_t[:, 0, c, :].bitcast(F32), ALU.subtract)\
                        .then_inc(g_free[g.xt[c]], 1)

            def choose():
                dve.wait_ge(s_gate_dve, seen(s_gate_dve, NT))
                for t in range(NT):
                    r = dve.max(top[:, t, :], scores_g[:, t, :])
                own(r)
                for t in range(NT):
                    r = dve.max_index(top_i[:, t, :], top[:, t, :], scores_g[:, t, :])
                own(r)
                own(dve.tensor_copy(chosen[:, :], top_i[:, :, 0]))
                for t in range(NT):
                    r = dve.tensor_scalar(onehot[:, t, :], expert_no[:, :], chosen[:, t:t + 1], None, ALU.is_equal)
                own(r)

            def rope_products(t):
                dve.wait_ge(s_qk_dve, seen(s_qk_dve))
                src = qk[:, t, :].rearrange("p (n h d) -> p n h d", n=2, h=2)
                for dst, table in ((qk_cos, t_cos), (qk_sin, t_sin)):
                    r = dve.tensor_tensor(dst[:, t, :].rearrange("p (n h d) -> p n h d", n=2, h=2), src,
                                          table[:, t, :, :].unsqueeze(2).to_broadcast([P, 2, 2, D]), ALU.mult)
                r.then_inc(s_products_pool, 1)
                dve.wait_ge(s_qk_dve, seen(s_qk_dve))
                r = dve.tensor_reduce(ss[:, t, :], qk_sq[:, t % 2, :, :], AX.X, ALU.add)
                r.then_inc(s_ss_pool, 1)
                if t < 2:
                    dve.drain().then_inc(s_sq_free, 1)

            def take_qk(g):
                for dst, i in ((k_t, g.kt), (q_t, g.qt)):
                    dve.wait_ge(s_qk_hi_dve, seen(s_qk_hi_dve))
                    dve.tensor_tensor(dst[:, 1, :], ps_g[i][:, :], dst[:, 0, :].bitcast(F32), ALU.subtract)\
                        .then_inc(g_free[i], 1)
                dve.tensor_scalar(q_scale[:, :, :], rms_inv[:, :, 0:2], SCALE * D, None, ALU.mult)

            def row_max(m):
                h, i = ITEMS[m]
                dve.wait_ge(s_scores_dve, seen(s_scores_dve))
                own(dve.tensor_reduce(neg_max[:, i, h:h + 1], ps_s[m % 2][:, 0:(i + 1) * P], AX.X, ALU.max, negate=True))
                dve.tensor_tensor(bias[:, i, h:h + 1], neg_max[:, i, h:h + 1], q_scale[:, i, h:h + 1], ALU.mult)\
                    .then_inc(s_bias_act, 1)

            def take_pt(m):
                w = (ITEMS[m][1] + 1) * P
                dve.wait_ge(s_pt_dve, seen(s_pt_dve))
                dve.tensor_copy(prob_t[:, m % 2, 0:w], ps_p[m % 2][:, 0:w]).then_inc(s_prob_t_dve, 1)

            def take_ot(hp, g):
                dve.wait_ge(s_ot_hi_dve, seen(s_ot_hi_dve))
                dve.tensor_tensor(o_t[:, 1, hp, :], ps_g[g.ot][:, :], o_t[:, 0, hp, :].bitcast(F32), ALU.subtract)\
                    .then_inc(g_free[g.ot], 1)

            def take_expert(t, hp, first, g):
                dve.wait_ge(s_expert_dve, seen(s_expert_dve))
                dve.scalar_tensor_tensor(acc[:, t, :], ps_g[g.exp[t]][:, 0:C], onehot[:, t, bass.ds(hp, 1)],
                                         res[:, t, :] if first else acc[:, t, :], ALU.mult, ALU.add)\
                    .then_inc(g_free[g.exp[t]], 1)

            def invert_sums():
                dve.wait_ge(s_o_dve, seen(s_o_dve))
                own(dve.reciprocal(row_inv[:, :, :], row_sum[:, :, :]))

            def normalise():
                dve.tensor_tensor(o_rows[:, :, :].rearrange("p t (h d) -> p (t h) d", d=D),
                                  ps_o[:, :].rearrange("p (n d) -> p n d", d=D),
                                  row_inv[:, :, :].rearrange("p t h -> p (t h)").unsqueeze(2).to_broadcast([P, NI, D]),
                                  ALU.mult).then_inc(s_o_pe, 1)

            def output(last, g):
                if last:
                    dve.wait_ge(s_out_stored, seen(s_out_stored, 16))
                else:
                    dve.wait_ge(s_res_dve, seen(s_res_dve))
                for half in range(2):
                    dve.wait_ge(s_proj_dve, seen(s_proj_dve))
                    rows = slice(2 * half, 2 * half + 2)
                    dve.tensor_tensor(out_sb[:, rows, :], ps_g[g.proj[half]][:, :].rearrange("p (t c) -> p t c", c=C),
                                      acc[:, rows, :], ALU.add).then_inc(g_free[g.proj[half]], 1)
                    if half == 0 and not last:
                        take_qk(g)
                dve.drain().then_inc(s_out_ready, 1)
                if not last:
                    dve.drain().then_inc(s_x_free, 1)

            dve.wait_ge(s_consts_dve, seen(s_consts_dve, 64))
            variances(row_stats(range(NT)))
            normalise_x()
            for table in (t_cos, t_sin):
                own(dve.tensor_copy(table[:, :, 1, :], table[:, :, 0, :]))
                for t in range(NT):
                    dve.tensor_tensor(table[:, t, :, :], table[:, t, :, :], nw[:, :, :], ALU.mult)
            for n, (dst, src) in enumerate(weight_chunks()):
                dve.wait_ge(w_loaded[n % 2], seen(w_loaded[n % 2], 16))
                w = staged[:, (n % 2) * chunk:(n % 2) * chunk + src.free_size()]
                own(dve.tensor_copy(dst[:, 0, :], w))
                dve.tensor_tensor(dst[:, 1, :], w, dst[:, 0, :].bitcast(F32), ALU.subtract).then_inc(s_w_free, 1)
            dve.drain().then_inc(s_weights_pe, 1)
            take_xt(LAST_PAIR_BANKS)
            for t in range(NT):
                rope_products(t)
            take_qk(LAST_PAIR_BANKS)
            dve.wait_ge(s_iota_dve, seen(s_iota_dve))
            dve.wait_ge(s_res_dve, seen(s_res_dve))
            dve.drain().then_inc(s_x_free, 1)
            row_max(0)
            seen.settle()

            def batch(b, last):
                def pair(hp, kind, hp_prev, hp_next, slot):
                    g, expert_steps, qkv_steps = plan(kind, last)
                    if kind == "last" and not last:
                        dve.wait_ge(s_x_loaded, seen(s_x_loaded, 16))
                    for step in range(STEPS):
                        m = step - 1
                        if 0 <= m < NI and m not in BY_ACT:
                            take_pt(m)
                        if step + 1 < NI:
                            row_max(step + 1)
                        if kind != "last" and step == QK_STEP:
                            take_qk(g)
                        if step - 1 in qkv_steps and step < STEPS - 1:
                            rope_products(qkv_steps[step - 1])
                        if step in expert_steps:
                            take_expert(expert_steps[step], hp, kind == "first", g)
                        if kind == "last" and not last:
                            if step in STATS_STEPS:
                                r = row_stats(STATS_STEPS[step])
                            if step == max(STATS_STEPS):
                                variances(r)
                            if step == NORM_STEP:
                                dve.wait_ge(s_out_stored, seen(s_out_stored, 16))
                                normalise_x()
                            if step == XT_STEP:
                                take_xt(g)
                        if kind != "first" and step == OT_STEP:
                            take_ot(hp_prev, g)
                        if kind == "first" and step == CHOOSE_STEP:
                            choose()
                    if kind == "last":
                        invert_sums()
                        normalise()
                        if not last:
                            rope_products(NT - 1)
                        take_ot(hp, OWN_OT)
                        output(last, g)
                        if not last:
                            row_max(0)
                    else:
                        invert_sums()
                        row_max(0)
                        normalise()
                        take_expert(NT - 1, hp, kind == "first", g)
                pairs(dve, pair, seen)

            batches(dve, batch)


def rope_tables(T, half):
    f = np.float32
    expo = (np.arange(0, 2 * half, 2, dtype=f) / f(2 * half)).astype(np.float64)
    inv = (1.0 / (10000.0 ** expo).astype(f).astype(np.float64)).astype(f)
    ang = (np.arange(T, dtype=f)[:, None] * inv).astype(np.float64)
    return np.cos(ang).astype(f), np.sin(ang).astype(f)


def kernel(**inputs):
    import concourse.bacc as bacc
    from concourse.bass_utils import run_bass_kernel_spmd

    x = np.ascontiguousarray(inputs["L0_attn_x"])
    B, T, C = x.shape
    nt, ncp = T // P, C // P
    wqkv = np.asarray(inputs["L0_attn_wqkv"])
    wqkv_t = wqkv.reshape(3, PAIRS, 2 * D, ncp, P).transpose(4, 3, 1, 0, 2).reshape(P, ncp, PAIRS * 6 * D)
    wo_t = np.asarray(inputs["L0_attn_wo"]).reshape(C, PAIRS, 2 * D).transpose(2, 1, 0)
    gate_w = np.asarray(inputs["L0_ffn_gate_w"])
    gate_t = gate_w.reshape(-1, ncp, P).transpose(2, 1, 0)
    wqkv_t = np.concatenate([gate_t, wqkv_t], axis=2)
    expert_t = np.asarray(inputs["L0_ffn_expert_w"]).reshape(-1, C, ncp, P).transpose(3, 2, 0, 1)
    norm_w = np.stack([np.asarray(inputs["L0_attn_q_norm_w"]), np.asarray(inputs["L0_attn_k_norm_w"])])
    norm_w = np.broadcast_to(norm_w, (P, 2, D))
    cos, sin = rope_tables(T, D // 2)
    rope_cos = np.concatenate([cos, cos], 1).reshape(nt, P, D).transpose(1, 0, 2)
    rope_sin = np.concatenate([sin, -sin], 1).reshape(nt, P, D).transpose(1, 0, 2)

    arrays = {
        "x": x, "wqkv_t": wqkv_t, "wo_t": wo_t, "norm_w": norm_w, "rope_cos": rope_cos, "rope_sin": rope_sin,
        "expert_t": expert_t,
    }
    arrays = {f"in_{k}": np.ascontiguousarray(a) for k, a in arrays.items()}
    nc = bacc.Bacc("TRN2", target_bir_lowering=False, num_devices=1)
    args = [nc.dram_tensor(k, a.shape, mybir.dt.from_np(a.dtype), kind="ExternalInput").ap() for k, a in arrays.items()]
    args.append(nc.dram_tensor("out", x.shape, F32, kind="ExternalOutput").ap())
    block_program(nc, *args)
    r = run_bass_kernel_spmd(nc, [arrays], core_ids=[0])
    return r.results[0]["out"]
```
